# Optimizing a Trainium2 kernel written in Bass

```python
import numpy as np
import jax
import jax.numpy as jnp

def _softmax(x, axis=-1):
    return jax.nn.softmax(x, axis=axis)

def _gelu(x):
    return jax.nn.gelu(x, approximate=True)

def _silu(x):
    return jax.nn.silu(x)

def _sigmoid(x):
    return jax.nn.sigmoid(x)

def _layernorm(x, axis=-1, eps=1e-05):
    m = jnp.mean(x, axis=axis, keepdims=True)
    v = jnp.var(x, axis=axis, keepdims=True)
    return (x - m) / jnp.sqrt(v + eps)

def _scatter_add(tgt, idx, src, axis=0):
    return tgt.at[idx].add(src)

def _segment_sum(src, seg, n):
    return jax.ops.segment_sum(src, seg, n)
kernel_name = 'mk_macaron_d1_jaxref_r8_d88169'

def setup_inputs(seed: int=0):
    np.random.seed(seed)
    _w = jnp.asarray

    def _L0_attn_setup():
        import jax, jax.numpy as jnp
        import numpy as np
        B, T, D = (8, 256, 128)
        H, N = (8, 32)

        def _xavier(key, shape, fan_in, fan_out):
            lim = float(np.sqrt(6.0 / (fan_in + fan_out)))
            return jax.random.uniform(key, shape, jnp.float32, -lim, lim)

        def _reference_tuple_inner(x, W_in, W_k, W_v, W_q, W_beta, b_beta, W_out):
            b, t, d = x.shape
            h, n = b_beta.shape
            xp = jax.nn.silu(jnp.einsum('btd,ed->bte', x, W_in))

            def proj(W):
                return jnp.einsum('btd,md->btm', xp, W).reshape(b, t, h, n).transpose(1, 0, 2, 3)
            k_all = proj(W_k)
            v_all = proj(W_v)
            q_all = proj(W_q)
            beta_all = jax.nn.sigmoid(proj(W_beta) + b_beta)
            S0 = jnp.zeros((b, h, n, n), x.dtype)

            def step(S, inp):
                k, v, q, beta = inp
                kn = k / (jnp.linalg.norm(k, axis=-1, keepdims=True) + 1e-06)
                retrieved = jnp.einsum('bhij,bhj->bhi', S, kn)
                delta = v - retrieved
                S = jnp.tanh(beta[..., None] * S + delta[..., None] * kn[..., None, :])
                Sq = jnp.einsum('bhij,bhj->bhi', S, q)
                out = Sq * jax.nn.silu(Sq)
                return (S, out)
            S_final, outs = jax.lax.scan(step, S0, (k_all, v_all, q_all, beta_all))
            cell_out = outs.transpose(1, 0, 2, 3).reshape(b, t, h * n)
            y = jnp.einsum('btm,dm->btd', cell_out, W_out)
            return (y, S_final)
        key = jax.random.key(seed)
        ks = jax.random.split(key, 8)
        x = jax.random.normal(ks[0], (B, T, D), jnp.float32)
        W_in = _xavier(ks[1], (D, D), D, D)
        W_k = _xavier(ks[2], (H * N, D), N, D)
        W_v = _xavier(ks[3], (H * N, D), N, D)
        W_q = _xavier(ks[4], (H * N, D), N, D)
        W_beta = _xavier(ks[5], (H * N, D), N, D)
        b_beta = jnp.full((H, N), 2.0, jnp.float32)
        W_out = _xavier(ks[6], (D, H * N), H * N, D)
        return {'x': x, 'W_in': W_in, 'W_k': W_k, 'W_v': W_v, 'W_q': W_q, 'W_beta': W_beta, 'b_beta': b_beta, 'W_out': W_out}
    _L0_attn_in = _L0_attn_setup()

    def _L0_ffn_setup():
        import jax, jax.numpy as jnp
        import numpy as np
        DIM = 128
        DEPTH = 6
        HEADS = 16
        DIM_HEAD = 64
        WINDOW = 32
        INNER = HEADS * DIM_HEAD
        DIM_INNER = int(DIM * 4 * 2 / 3)
        QK_SCALE = 8.0

        def shift_tokens(t):
            a, s = jnp.split(t, 2, -1)
            s = jnp.pad(s, ((0, 0), (1, 0), (0, 0)))[:, :-1]
            return jnp.concatenate([a, s], -1)

        def l2norm(t):
            return t / jnp.maximum(jnp.linalg.norm(t, axis=-1, keepdims=True), 1e-12)

        def rotate_half(x):
            x1, x2 = jnp.split(x, 2, -1)
            return jnp.concatenate([-x2, x1], -1)

        def rotary_tables(n):
            half = jnp.arange(0, DIM_HEAD, 2, dtype=jnp.float32)
            inv_freq = 1.0 / 10000.0 ** (half / DIM_HEAD)
            t = jnp.arange(n, dtype=jnp.float32)
            freqs = t[:, None] * inv_freq[None, :]
            freqs = jnp.concatenate([freqs, freqs], -1)
            base_scale = (half + 0.4 * DIM_HEAD) / (1.4 * DIM_HEAD)
            power = (t - n // 2) / (WINDOW // 2)
            scale = base_scale[None, :] ** power[:, None]
            scale = jnp.concatenate([scale, scale], -1)
            return (freqs, scale)

        def local_attention(q, k, v):
            b, h, n, d = q.shape
            w = WINDOW
            nw = n // w
            bq = q.reshape(b, h, nw, w, d)
            bk = k.reshape(b, h, nw, w, d)
            bv = v.reshape(b, h, nw, w, d)

            def look(t):
                p = jnp.pad(t, ((0, 0), (0, 0), (1, 0), (0, 0), (0, 0)))
                return jnp.concatenate([p[:, :, :nw], p[:, :, 1:]], axis=3)
            bk2, bv2 = (look(bk), look(bv))
            seq = jnp.arange(n).reshape(nw, w)
            seq_p = jnp.pad(seq, ((1, 0), (0, 0)), constant_values=-1)
            jt = jnp.concatenate([seq_p[:nw], seq_p[1:]], axis=1)
            it = seq[:, :, None]
            jb = jt[:, None, :]
            mask = (it < jb) | (it > jb + w) | (jb == -1)
            sim = jnp.einsum('bhwie,bhwje->bhwij', bq, bk2) * QK_SCALE
            sim = jnp.where(mask, -jnp.finfo(sim.dtype).max, sim)
            attn = jax.nn.softmax(sim, -1)
            out = jnp.einsum('bhwij,bhwje->bhwie', attn, bv2)
            return out.reshape(b, h, n, d)

        def attn_layer(x, Wqkv, qs, ksc, Wo):
            b, n, _ = x.shape
            qkv = x @ Wqkv
            q, k, v = jnp.split(qkv, 3, -1)
            sh = lambda t: t.reshape(b, n, HEADS, DIM_HEAD).transpose(0, 2, 1, 3)
            q, k, v = (sh(q), sh(k), sh(v))
            q = l2norm(q) * qs
            k = l2norm(k) * ksc
            freqs, scale = rotary_tables(n)
            cos, sin = (jnp.cos(freqs), jnp.sin(freqs))
            q = q * cos * scale + rotate_half(q) * sin * scale
            inv = 1.0 / scale
            k = k * cos * inv + rotate_half(k) * sin * inv
            out = local_attention(q, k, v)
            out = out.transpose(0, 2, 1, 3).reshape(b, n, INNER)
            return out @ Wo

        def ffn_layer(x, g, bln, W1, b1, W2, b2):
            mu = x.mean(-1, keepdims=True)
            var = ((x - mu) ** 2).mean(-1, keepdims=True)
            xn = (x - mu) / jnp.sqrt(var + 1e-05) * g + bln
            hg = xn @ W1 + b1
            a, gate = jnp.split(hg, 2, -1)
            return a * jax.nn.gelu(gate, approximate=False) @ W2 + b2
        key = jax.random.key(seed)
        ks = jax.random.split(key, 8)
        B, N = (2, 256)
        init = lambda k, shape: jax.random.normal(k, shape, jnp.float32) * 0.02
        return {'x': jax.random.normal(ks[0], (B, N, DIM), jnp.float32), 'Wqkv': init(ks[1], (DEPTH, DIM, 3 * INNER)), 'q_scale': jnp.ones((DEPTH, DIM_HEAD), jnp.float32), 'k_scale': jnp.ones((DEPTH, DIM_HEAD), jnp.float32), 'Wo': init(ks[2], (DEPTH, INNER, DIM)), 'ln_g': jnp.ones((DEPTH, DIM), jnp.float32), 'ln_b': jnp.zeros((DEPTH, DIM), jnp.float32), 'W1': init(ks[3], (DEPTH, DIM, 2 * DIM_INNER)), 'b1': jnp.zeros((DEPTH, 2 * DIM_INNER), jnp.float32), 'W2': init(ks[4], (DEPTH, DIM_INNER, DIM)), 'b2': jnp.zeros((DEPTH, DIM), jnp.float32)}
    _L0_ffn_in = _L0_ffn_setup()
    _d = {'L0_attn_x': _L0_attn_in['x'], 'L0_attn_W_in': _L0_attn_in['W_in'], 'L0_attn_W_k': _L0_attn_in['W_k'], 'L0_attn_W_v': _L0_attn_in['W_v'], 'L0_attn_W_q': _L0_attn_in['W_q'], 'L0_attn_W_beta': _L0_attn_in['W_beta'], 'L0_attn_b_beta': _L0_attn_in['b_beta'], 'L0_attn_W_out': _L0_attn_in['W_out'], 'L0_ffn_Wqkv': _L0_ffn_in['Wqkv'], 'L0_ffn_q_scale': _L0_ffn_in['q_scale'], 'L0_ffn_k_scale': _L0_ffn_in['k_scale'], 'L0_ffn_Wo': _L0_ffn_in['Wo'], 'L0_ffn_ln_g': _L0_ffn_in['ln_g'], 'L0_ffn_ln_b': _L0_ffn_in['ln_b'], 'L0_ffn_W1': _L0_ffn_in['W1'], 'L0_ffn_b1': _L0_ffn_in['b1'], 'L0_ffn_W2': _L0_ffn_in['W2'], 'L0_ffn_b2': _L0_ffn_in['b2']}
    _x0 = _d['L0_attn_x']
    _d['L0_attn_x'] = jax.random.normal(jax.random.fold_in(jax.random.key(seed), 1), (2, 1024, 128), dtype=_x0.dtype)
    del _x0
    return _d

def reference(L0_attn_x, L0_attn_W_in, L0_attn_W_k, L0_attn_W_v, L0_attn_W_q, L0_attn_W_beta, L0_attn_b_beta, L0_attn_W_out, L0_ffn_Wqkv, L0_ffn_q_scale, L0_ffn_k_scale, L0_ffn_Wo, L0_ffn_ln_g, L0_ffn_ln_b, L0_ffn_W1, L0_ffn_b1, L0_ffn_W2, L0_ffn_b2):

    def _L0_attn_ref(x, W_in, W_k, W_v, W_q, W_beta, b_beta, W_out):
        import jax, jax.numpy as jnp
        import numpy as np
        B, T, D = (8, 256, 128)
        H, N = (8, 32)

        def _xavier(key, shape, fan_in, fan_out):
            lim = float(np.sqrt(6.0 / (fan_in + fan_out)))
            return jax.random.uniform(key, shape, jnp.float32, -lim, lim)

        def _reference_tuple_inner(x, W_in, W_k, W_v, W_q, W_beta, b_beta, W_out):
            b, t, d = x.shape
            h, n = b_beta.shape
            xp = jax.nn.silu(jnp.einsum('btd,ed->bte', x, W_in))

            def proj(W):
                return jnp.einsum('btd,md->btm', xp, W).reshape(b, t, h, n).transpose(1, 0, 2, 3)
            k_all = proj(W_k)
            v_all = proj(W_v)
            q_all = proj(W_q)
            beta_all = jax.nn.sigmoid(proj(W_beta) + b_beta)
            S0 = jnp.zeros((b, h, n, n), x.dtype)

            def step(S, inp):
                k, v, q, beta = inp
                kn = k / (jnp.linalg.norm(k, axis=-1, keepdims=True) + 1e-06)
                retrieved = jnp.einsum('bhij,bhj->bhi', S, kn)
                delta = v - retrieved
                S = jnp.tanh(beta[..., None] * S + delta[..., None] * kn[..., None, :])
                Sq = jnp.einsum('bhij,bhj->bhi', S, q)
                out = Sq * jax.nn.silu(Sq)
                return (S, out)
            S_final, outs = jax.lax.scan(step, S0, (k_all, v_all, q_all, beta_all))
            cell_out = outs.transpose(1, 0, 2, 3).reshape(b, t, h * n)
            y = jnp.einsum('btm,dm->btd', cell_out, W_out)
            return (y, S_final)
        return _reference_tuple_inner(x, W_in, W_k, W_v, W_q, W_beta, b_beta, W_out)[0]

    def _L0_ffn_ref(x, Wqkv, q_scale, k_scale, Wo, ln_g, ln_b, W1, b1, W2, b2):
        import jax, jax.numpy as jnp
        import numpy as np
        DIM = 128
        DEPTH = 6
        HEADS = 16
        DIM_HEAD = 64
        WINDOW = 32
        INNER = HEADS * DIM_HEAD
        DIM_INNER = int(DIM * 4 * 2 / 3)
        QK_SCALE = 8.0

        def shift_tokens(t):
            a, s = jnp.split(t, 2, -1)
            s = jnp.pad(s, ((0, 0), (1, 0), (0, 0)))[:, :-1]
            return jnp.concatenate([a, s], -1)

        def l2norm(t):
            return t / jnp.maximum(jnp.linalg.norm(t, axis=-1, keepdims=True), 1e-12)

        def rotate_half(x):
            x1, x2 = jnp.split(x, 2, -1)
            return jnp.concatenate([-x2, x1], -1)

        def rotary_tables(n):
            half = jnp.arange(0, DIM_HEAD, 2, dtype=jnp.float32)
            inv_freq = 1.0 / 10000.0 ** (half / DIM_HEAD)
            t = jnp.arange(n, dtype=jnp.float32)
            freqs = t[:, None] * inv_freq[None, :]
            freqs = jnp.concatenate([freqs, freqs], -1)
            base_scale = (half + 0.4 * DIM_HEAD) / (1.4 * DIM_HEAD)
            power = (t - n // 2) / (WINDOW // 2)
            scale = base_scale[None, :] ** power[:, None]
            scale = jnp.concatenate([scale, scale], -1)
            return (freqs, scale)

        def local_attention(q, k, v):
            b, h, n, d = q.shape
            w = WINDOW
            nw = n // w
            bq = q.reshape(b, h, nw, w, d)
            bk = k.reshape(b, h, nw, w, d)
            bv = v.reshape(b, h, nw, w, d)

            def look(t):
                p = jnp.pad(t, ((0, 0), (0, 0), (1, 0), (0, 0), (0, 0)))
                return jnp.concatenate([p[:, :, :nw], p[:, :, 1:]], axis=3)
            bk2, bv2 = (look(bk), look(bv))
            seq = jnp.arange(n).reshape(nw, w)
            seq_p = jnp.pad(seq, ((1, 0), (0, 0)), constant_values=-1)
            jt = jnp.concatenate([seq_p[:nw], seq_p[1:]], axis=1)
            it = seq[:, :, None]
            jb = jt[:, None, :]
            mask = (it < jb) | (it > jb + w) | (jb == -1)
            sim = jnp.einsum('bhwie,bhwje->bhwij', bq, bk2) * QK_SCALE
            sim = jnp.where(mask, -jnp.finfo(sim.dtype).max, sim)
            attn = jax.nn.softmax(sim, -1)
            out = jnp.einsum('bhwij,bhwje->bhwie', attn, bv2)
            return out.reshape(b, h, n, d)

        def attn_layer(x, Wqkv, qs, ksc, Wo):
            b, n, _ = x.shape
            qkv = x @ Wqkv
            q, k, v = jnp.split(qkv, 3, -1)
            sh = lambda t: t.reshape(b, n, HEADS, DIM_HEAD).transpose(0, 2, 1, 3)
            q, k, v = (sh(q), sh(k), sh(v))
            q = l2norm(q) * qs
            k = l2norm(k) * ksc
            freqs, scale = rotary_tables(n)
            cos, sin = (jnp.cos(freqs), jnp.sin(freqs))
            q = q * cos * scale + rotate_half(q) * sin * scale
            inv = 1.0 / scale
            k = k * cos * inv + rotate_half(k) * sin * inv
            out = local_attention(q, k, v)
            out = out.transpose(0, 2, 1, 3).reshape(b, n, INNER)
            return out @ Wo

        def ffn_layer(x, g, bln, W1, b1, W2, b2):
            mu = x.mean(-1, keepdims=True)
            var = ((x - mu) ** 2).mean(-1, keepdims=True)
            xn = (x - mu) / jnp.sqrt(var + 1e-05) * g + bln
            hg = xn @ W1 + b1
            a, gate = jnp.split(hg, 2, -1)
            return a * jax.nn.gelu(gate, approximate=False) @ W2 + b2
        for i in range(DEPTH):
            x = attn_layer(shift_tokens(x), Wqkv[i], q_scale[i], k_scale[i], Wo[i]) + x
            x = ffn_layer(shift_tokens(x), ln_g[i], ln_b[i], W1[i], b1[i], W2[i], b2[i]) + x
        return x
    x = L0_attn_x
    x = x + 0.5 * _L0_ffn_ref(_layernorm(x, axis=-1), L0_ffn_Wqkv, L0_ffn_q_scale, L0_ffn_k_scale, L0_ffn_Wo, L0_ffn_ln_g, L0_ffn_ln_b, L0_ffn_W1, L0_ffn_b1, L0_ffn_W2, L0_ffn_b2)
    x = x + _L0_attn_ref(_layernorm(x, axis=-1), L0_attn_W_in, L0_attn_W_k, L0_attn_W_v, L0_attn_W_q, L0_attn_W_beta, L0_attn_b_beta, L0_attn_W_out)
    x = x + 0.5 * _L0_ffn_ref(_layernorm(x, axis=-1), L0_ffn_Wqkv, L0_ffn_q_scale, L0_ffn_k_scale, L0_ffn_Wo, L0_ffn_ln_g, L0_ffn_ln_b, L0_ffn_W1, L0_ffn_b1, L0_ffn_W2, L0_ffn_b2)
    return x

_drawn_inputs = setup_inputs


def setup_inputs(seed=0):
    import zlib

    import numpy as np

    out = dict(_drawn_inputs(seed))
    spreads = {'L0_attn_b_beta': (2.0, 0.2),
     'L0_ffn_q_scale': (1.0, 0.6),
     'L0_ffn_k_scale': (1.0, 0.6),
     'L0_ffn_ln_g': (1.0, 0.6),
     'L0_ffn_ln_b': (0.0, 0.8),
     'L0_ffn_b1': (0.0, 0.8),
     'L0_ffn_b2': (0.0, 0.1)}
    factors = {'L0_ffn_W1': 3.771, 'L0_ffn_W2': 3.701}
    for name, (base, spread) in spreads.items():
        noise = np.random.default_rng([zlib.crc32(name.encode()), seed]).standard_normal(out[name].shape)
        drawn = base * np.exp(spread * noise) if base else spread * noise
        out[name] = jnp.asarray(drawn.astype(out[name].dtype))
    for name, factor in factors.items():
        out[name] = (out[name] * factor).astype(out[name].dtype)
    return out
```

```python
from contextlib import ExitStack

import numpy as np

import concourse.bass as bass
from concourse import mybir

F32 = mybir.dt.float32
I32 = mybir.dt.int32
U32 = mybir.dt.uint32
ALU = mybir.AluOpType
ACT = mybir.ActivationFunctionType
AX_X = mybir.AxisListType.X

P = 128
DIM = 128
LAYERS = 6
HEADS, DH = 16, 64
WIN = 32
INNER = HEADS * DH
PAIRS = HEADS // 2
FF = int(DIM * 4 * 2 / 3)
RH, RN = 8, 32
RG = RH * RN // P
UNROLL, BLOCK = 8, 4
FF_CUTS = [(0, 128), (128, 256), (256, FF)]
LN_EPS = 1e-5
BANK = 512
RSQRT_MAGIC = float(0x5F3759DF)

ORDER = [("turn", 0), ("score", 0), ("turn", 1), ("soft", 0), ("score", 1), ("load", 0), ("qk", 0),
         ("soft", 1), ("pturn", 0), ("pv", 0), ("v", 0), ("wo", 0), ("norm", 0), ("load", 1), ("qk", 1),
         ("ln", 0), ("cent", 0), ("rope", 0), ("var", 0), ("pturn", 1), ("pv", 1), ("v", 1), ("wo", 1),
         ("up", 0), ("ln", 1), ("cent", 1), ("norm", 1), ("var", 1), ("gturn", 0), ("up", 1), ("down", 0), ("gturn", 1),
         ("rope", 1), ("down", 1)]
AHEAD = ("load", "qk", "norm", "rope", "v")
RING_USES = {"turn": 4, "qk": 4, "pturn": 4, "v": 2}


def ring_offsets(order):
    at, out = 0, {}
    for name, b in order:
        if name in RING_USES:
            out[name, b] = at
            at += RING_USES[name]
    return out, at


FIRST = [s for s in ORDER if s[0] in AHEAD]
RING_AT, RING_N = ring_offsets(ORDER)
RING_AT0, RING_N0 = ring_offsets(FIRST)


ARENA = 23360


def build(nc, x, tables, mask, ident_in, spread_in, W_in, W_k, W_v, W_q, W_beta, b_beta, W_out,
          Wqkv, q_scale, k_scale, Wo, ln_g, ln_b, W1, b1, W2, b2, out, layers=LAYERS, phases=2):
    B, T, _ = x.shape
    POS = T // P
    SLOTS = POS * B
    ITERS = layers * POS
    A_N, B_N = 2 * (ITERS + 1), 2 * ITERS
    X_N = SLOTS + B_N
    X_BASE = [0, X_N + SLOTS]
    R_N = RING_N0 + RING_N * ITERS

    with ExitStack() as ctx:
        def sb(name, shape, dt=F32):
            return ctx.enter_context(nc.sbuf_tensor(name, shape, dt))

        def sem(name):
            return ctx.enter_context(nc.semaphore(name))

        arena = sb("arena", [P, ARENA])

        def carver(start=0):
            at = [start]

            def cut(shape):
                n = int(np.prod(shape[1:]))
                a, at[0] = at[0], at[0] + n
                assert at[0] <= ARENA, at[0]
                v = arena[0:shape[0], a:a + n]
                if len(shape) == 2:
                    return v
                names = "abcde"[:len(shape) - 1]
                return v.rearrange(f"p ({' '.join(names)}) -> p {' '.join(names)}",
                                   **dict(zip(names[1:], shape[2:])))
            cut.at = at
            return cut

        ffn, rec = carver(), carver()
        x_in = sb("x_in", [P, SLOTS, DIM])
        x_tok = sb("x_tok", [P, SLOTS, DIM])
        wqkv = sb("wqkv", [DIM, 2, 3 * INNER])
        wo = sb("wo", [P, 2, PAIRS, DIM])
        w1 = sb("w1", [DIM, 2, 2 * FF])
        w2 = sb("w2", [P, 2, 3, DIM])
        b1r = sb("b1r", [1, 2, 2 * FF])
        b2r = sb("b2r", [1, 2, DIM])
        scales = sb("scales", [P, 2, 4, DH])
        rope_base = sb("rope_base", [P, POS, 4, DH])
        rope_tab = sb("rope_tab", [P, 2, 4, DH])
        masks = sb("masks", [P, 2, 2 * WIN])
        gcol = sb("gcol", [DIM, layers])
        bcol = sb("bcol", [DIM, layers])
        ident = sb("ident", [P, P])
        center = sb("center", [P, P])
        ones = sb("ones", [P, P])
        mean_col = sb("mean_col", [P, 1])
        bbc = sb("bbc", [P, P])
        up_bias = sb("up_bias", [P, 2 * FF])
        xcur = ffn([P, 2, DIM])
        xs = sb("xs", [P, 2, P + 2])
        fs = sb("fs", [P, 2, P + 2])
        qk = ffn([P, 2, 2 * INNER])
        scr = ffn([P, 2, 2 * INNER])
        rot = ffn([P, 2 * INNER])
        ss = ffn([P, 2, 2 * HEADS])
        qT = ffn([P, 2, PAIRS, P])
        kT = sb("kT", [P, 2, PAIRS, WIN + P + WIN])
        v_al = ffn([P, 2, INNER])
        v_sh = ffn([P, 2, INNER])
        sm = ffn([P, 2 * PAIRS, 2 * WIN])
        mx = ffn([P, HEADS])
        rl = ffn([P, HEADS])
        p_pad = sb("p_pad", [P, HEADS, P])
        pT = ffn([P, HEADS, P])
        oT = ffn([P, PAIRS, P])
        xmid = ffn([P, 2, DIM])
        cg = ffn([P, 2, P])
        csq = ffn([P, 2, P])
        rstd = ffn([P, 2])
        ag = ffn([P, 2, 2 * FF])
        gT = ffn([P, 3, P])
        nt = sb("nt", [P, 3, 2 * HEADS])
        stats = sb("stats", [P, SLOTS, 6])
        mv = sb("mv", [P, SLOTS, 2])
        rs16 = sb("rs16", [P, SLOTS])

        GR = B * RG
        w_t = rec([P, 11, P])
        v_neg = rec([P, T, GR])
        beta = rec([P, T, GR])
        beta_bias = rec([P, RG])
        spread = rec([4, P])
        prep, loop = carver(rec.at[0]), carver(rec.at[0])
        w_raw = prep([P, 11, P])
        xT = prep([P, SLOTS * P])
        xpT = prep([P, SLOTS * P])
        kq = prep([P, SLOTS // 2, 2, RH * RN])
        ksq = prep([P, SLOTS // 2, RH * RN])
        knorm = prep([P, SLOTS // 2 * RH])
        nt_r = prep([P, 3, SLOTS // 2 * RH])
        kq_in = loop([4, 2, 2, UNROLL * GR * RN])
        sq = loop([P, BLOCK + T, GR])
        keys = loop([P, UNROLL, GR, RN + 1])
        hist = loop([P, UNROLL, GR, RN + 1])
        prod = loop([P, B, RG, RN + 1])
        nd = loop([P, B, RG])
        upd = loop([P, B, RG, RN])
        decay = loop([P, B, RG, RN])
        arg = loop([P, B, RG, RN])
        qprod = loop([P, BLOCK * GR, RN])
        gate = carver(rec.at[0])([P, T, GR])

        ring = [ctx.enter_context(nc.psum_tensor(f"ring{j}", [P, BANK], F32)) for j in range(2)]
        psS = ctx.enter_context(nc.psum_tensor("psS", [P, 2 * BANK], F32))
        psO = ctx.enter_context(nc.psum_tensor("psO", [P, 2 * BANK], F32))
        psM = [ctx.enter_context(nc.psum_tensor(f"psM{j}", [P, BANK], F32)) for j in range(2)]

        in_x = sem("in_x")
        in_const = sem("in_const")
        in_w = sem("in_w")
        consts = sem("consts")
        x_done = sem("x_done")
        dve = sem("dve")
        x_copied = sem("x_copied")
        x_turned = sem("x_turned")
        xs_ready = sem("xs_ready")
        xs_carry = sem("xs_carry")
        fs_carry = sem("fs_carry")
        ring_full = sem("ring_full")
        chunk_out = sem("chunk_out")
        qn_ready = sem("qn_ready")
        rt_ready = sem("rt_ready")
        rs_ready = sem("rs_ready")
        rot_ready = sem("rot_ready")
        tail_copied = sem("tail_copied")
        s_done = sem("s_done")
        s_read = sem("s_read")
        sub_done = sem("sub_done")
        exp_done = sem("exp_done")
        p_ready = sem("p_ready")
        pv_done = sem("pv_done")
        oT_ready = sem("oT_ready")
        v_edge = sem("v_edge")
        v_rest = sem("v_rest")
        y_done = sem("y_done")
        xmid_ready = sem("xmid_ready")
        m_turned = sem("m_turned")
        fs_ready = sem("fs_ready")
        c_done = sem("c_done")
        c_ready = sem("c_ready")
        var_done = sem("var_done")
        up_done = sem("up_done")
        gate_ready = sem("gate_ready")
        gelu_done = sem("gelu_done")
        g_ready = sem("g_ready")
        g_turned = sem("g_turned")
        gT_ready = sem("gT_ready")
        y2_done = sem("y2_done")
        bb_ready = sem("bb_ready")
        ub_done = sem("ub_done")
        ub_ready = sem("ub_ready")
        in_r = sem("in_r")
        piece_full = sem("piece_full")
        piece_out = sem("piece_out")
        kn_ready = sem("kn_ready")
        kq_stored = sem("kq_stored")
        in_kq = sem("in_kq")
        k_spread = sem("k_spread")
        q_spread = sem("q_spread")
        keys_ready = sem("keys_ready")
        q_used = sem("q_used")
        sq_ready = sem("sq_ready")
        state = sem("state")
        decayed = sem("decayed")
        arg_ready = sem("arg_ready")
        rdve = sem("rdve")
        gate_r = sem("gate_r")
        cell = sem("cell")
        cell_y = sem("cell_y")
        apart = {nc.tensor: sem("apart_pe"), nc.gpsimd: sem("apart_pool")}
        s_out = sem("s_out")
        fin = sem("fin")

        W_DMAS = 14
        C_DMAS = 5
        CONSTS = 8

        LINKS = {"norm": 5 + 12, "rope": 1, "soft": 3, "var": 1 + 12}
        links_at, links_n = {}, 0
        for step in ORDER:
            links_at[step] = links_n
            links_n += LINKS.get(step[0], 0)
        links_at0, links_n0 = {}, 0
        for step in FIRST:
            links_at0[step] = links_n0
            links_n0 += LINKS.get(step[0], 0)
        LN_LINKS = 3 + 12
        D_N = LN_LINKS + links_n0 + links_n * ITERS
        D_BASE = [0, D_N + LN_LINKS]

        def nA(ph, i1, b):
            return i1 * 2 + (A_N * ph + b)

        def nB(ph, i, b):
            return i * 2 + (B_N * ph + b)

        def ring_base(ph, i):
            return i * RING_N + (R_N * ph + RING_N0)

        def earlier(name, step):
            return sum(s[0] == name for s in ORDER[:ORDER.index(step)])

        def loads_of(ph, l):
            return l * (16 * W_DMAS) + 16 * W_DMAS * (layers * ph + 1)

        def slot_of(i, b):
            return (i % POS) * B + b

        def par(i):
            return (i // POS) % 2

        kq_dram = nc.dram_tensor("kq_dram", [2, 4, T, GR, RN], F32, kind="Internal").ap()
        R_ITERS = T // UNROLL
        HALVES = UNROLL // BLOCK
        BCOLS = BLOCK * GR * RN
        N_PIECES = [3, SLOTS // 4, SLOTS // 4, RG * SLOTS // 4, RG * SLOTS // 4, SLOTS]
        PIECE = [sum(N_PIECES[:n]) for n in range(len(N_PIECES) + 1)]
        R_DMAS = 8
        STORES = SLOTS // 2 * 2 * RG

        def wait_apart(eng, *waits):
            for sem_, v in waits:
                eng.wait_ge(sem_, v)
            eng.sem_inc(apart[eng], 1)

        def ffn_over(eng):
            eng.wait_ge(fin, 1)
            eng.wait_ge(rot_ready, A_N)
            eng.wait_ge(v_rest, 16 * A_N)
            eng.wait_ge(chunk_out, R_N)

        START = 1
        early = {nc.tensor: (y_done, y2_done, ub_done), nc.scalar: (oT_ready, fs_ready, keys_ready),
                 nc.vector: (s_read, p_ready, gate_ready, arg_ready, sq_ready)}

        block = ctx.enter_context(nc.Block())

        @block.sync
        def _(sp):
            def load_layer(l, half):
                def put(dst, src):
                    sp.dma_start(dst, src).then_inc(in_w, 16)
                at, ly = bass.ds(half, 1), bass.ds(l, 1)
                put(wqkv[:, at, :], Wqkv[ly].rearrange("l d n -> d l n"))
                put(wo[:, at, :, :].rearrange("p s k n -> p (s k) n"), Wo[ly].rearrange("l (k p) n -> p (l k) n", p=P))
                put(w1[:, at, :], W1[ly].rearrange("l d n -> d l n"))
                for j, (a, z) in enumerate(FF_CUTS):
                    put(w2[0:z - a, at, j, :], W2[ly, a:z, :].rearrange("l f n -> f l n"))
                put(b1r[:, at, :], b1[ly, :].unsqueeze(0))
                put(b2r[:, at, :], b2[ly, :].unsqueeze(0))
                h = DH // 2
                for j, vec in enumerate((q_scale, k_scale)):
                    put(scales[:, at, j, :], vec[ly, :].partition_broadcast(P))
                    put(scales[:, at, 2 + j, 0:h], vec[ly, h:DH].partition_broadcast(P))
                    put(scales[:, at, 2 + j, h:DH], vec[ly, 0:h].partition_broadcast(P))

            def v_shift(ph, i1, b, rb, first=False):
                n = nA(ph, i1, b)
                if first and ph == 0:
                    sp.wait_ge(consts, CONSTS)
                else:
                    sp.wait_ge(pv_done, nB(ph, i1 - 1, b) + 1)
                sp.dma_start(v_sh[0:WIN, b, :], v_al[P - WIN:P, b, :]).then_inc(v_edge, 16)
                sp.wait_ge(chunk_out, rb + 2)
                sp.dma_start(v_sh[WIN:P, b, :], v_al[0:P - WIN, b, :]).then_inc(v_rest, 16)

            for b in range(B):
                sp.dma_start(x_in[:, b::B, :], x[b].rearrange("(s t) d -> t s d", t=P)).then_inc(in_x, 16)
            sp.dma_start(ident[:, :], ident_in).then_inc(in_const, 16)
            sp.dma_start(rope_base[:, :, :, :], tables).then_inc(in_const, 16)
            sp.dma_start(masks[:, :, :], mask).then_inc(in_const, 16)
            with nc.allow_non_contiguous_dma("a few columns"):
                sp.dma_start(gcol[:, :], ln_g[0:layers].rearrange("l d -> d l")).then_inc(in_const, 16)
                sp.dma_start(bcol[:, :], ln_b[0:layers].rearrange("l d -> d l")).then_inc(in_const, 16)
            load_layer(0, 0)
            def recurrence():
                ffn_over(sp)
                sp.dma_start(w_raw[:, 0, :], W_in).then_inc(in_r, 16)
                for j, w in enumerate((W_k, W_q, W_v, W_beta)):
                    sp.dma_start(w_raw[:, 1 + 2 * j:3 + 2 * j, :], w.rearrange("(g m) d -> m g d", g=RG)).then_inc(in_r, 16)
                sp.dma_start(w_raw[:, 9:11, :], W_out.rearrange("d (g m) -> d g m", g=RG)).then_inc(in_r, 16)
                with nc.allow_non_contiguous_dma("two columns"):
                    sp.dma_start(beta_bias, b_beta.rearrange("(g h) n -> (h n) g", g=RG)).then_inc(in_r, 16)
                sp.dma_start(spread, spread_in).then_inc(in_r, 16)
                for hf in range(2):
                    sp.wait_ge(kn_ready, hf + 1)
                    for n in range(SLOTS // 2):
                        slot = hf * (SLOTS // 2) + n
                        ps, b = slot // B, slot % B
                        for a in range(2):
                            for g in range(RG):
                                sp.dma_start(kq_dram[a, :, ps * P:(ps + 1) * P, b * RG + g, :].rearrange("h t j -> t h j"),
                                             kq[:, n, a, g * P:(g + 1) * P].rearrange("t (h j) -> t h j", j=RN)
                                             ).then_inc(kq_stored, 16)
                kq_rows = kq_dram.rearrange("a h t g j -> h a (t g j)")

                def load(it):
                    sp.dma_start(kq_in[:, bass.ds(it % 2, 1), :, :].rearrange("h r a n -> h (r a) n"),
                                 kq_rows[:, :, bass.ds((it % R_ITERS) * (UNROLL * GR * RN), UNROLL * GR * RN)]).then_inc(in_kq, 16)
                sp.wait_ge(kq_stored, 16 * 2 * STORES)
                load(0)
                with sp.Fori(0, R_ITERS) as it:
                    sp.wait_ge(q_spread, it * HALVES + 1)
                    sp.wait_ge(in_kq, it * 16 + 16)
                    load(it + 1)

            for ph in range(phases):
                if ph:
                    recurrence()
                    sp.wait_ge(fin, 2)
                for step in FIRST:
                    if step[0] == "v":
                        v_shift(ph, 0, step[1], R_N * ph + RING_AT0[step], first=True)
                with sp.Fori(0, layers) as l:
                    sp.wait_ge(y2_done, l * (2 * POS) + B_N * ph + START)
                    load_layer((l + 1) % layers, (l + 1) % 2)
                    with sp.Fori(0, POS) as p:
                        i = l * POS + p
                        for step in ORDER:
                            if step[0] == "v":
                                v_shift(ph, i + 1, step[1], ring_base(ph, i) + RING_AT[step])
            sp.wait_ge(fin, 2 * phases - 1)
            for b in range(B):
                sp.dma_start(out[b].rearrange("(s t) d -> t s d", t=P), x_in[:, b::B, :]).then_inc(s_out, 16)
            sp.wait_ge(s_out, 16 * B)

        @block.gpsimd
        def _(pool):
            def rope(ph, i1, b, rb, first=False):
                n = nA(ph, i1, b)
                if b == 0:
                    pool.wait_ge(in_w, loads_of(ph, i1 // POS))
                    if not first:
                        pool.wait_ge(rot_ready, nA(ph, i1 - 1, 0))
                    elif ph:
                        pool.wait_ge(rot_ready, nA(ph, 0, 0))
                        pool.wait_ge(rs_ready, nA(ph, 0, 0) * 4)
                    pool.tensor_tensor(rope_tab[:, bass.ds(i1 % 2, 1)], rope_base[:, bass.ds(i1 % POS, 1)],
                                       scales[:, bass.ds(par(i1), 1)], ALU.mult).then_inc(rt_ready, 1)
                    pool.wait_ge(rt_ready, i1 + (ITERS + 1) * ph + 1)
                wait_apart(pool, (qn_ready, n + 1), *([] if first and ph == 0 and b == 0 else [(rot_ready, n)]))
                h = DH // 2
                src = qk[:, b, :].rearrange("p (t h d) -> p t h d", t=2, d=DH)
                dst = rot[:, :].rearrange("p (t h d) -> p t h d", t=2, d=DH)
                for a, z in ((0, h), (h, DH)):
                    for t in range(2):
                        tab = rope_tab[:, bass.ds(i1 % 2, 1), 2 + t, a:z].broadcast_to([P, HEADS, h])
                        pool.tensor_tensor(dst[:, t, :, a:z], src[:, t, :, h - a:DH - a], tab,
                                           ALU.mult).then_inc(rs_ready, 1)

            pool.memset(ones[:, :], 1.0).then_inc(consts, 1)
            pool.memset(kT[:, :, :, :], 0.0).then_inc(consts, 1)
            pool.memset(v_al[:, :, :], 0.0).then_inc(consts, 1)
            pool.memset(p_pad[:, :, :], 0.0).then_inc(consts, 1)
            pool.memset(xs[:, :, P:P + 2], 0.0).then_inc(consts, 1)
            pool.memset(fs[:, :, P:P + 2], 0.0).then_inc(consts, 1)
            pool.memset(mean_col[:, :], 1.0 / DIM).then_inc(consts, 1)
            pool.wait_ge(in_const, 16 * C_DMAS)
            pool.tensor_scalar(center[:, :], ident[:, :], 1.0 / DIM, None, ALU.subtract).then_inc(consts, 1)
            def recurrence():
                ffn_over(pool)
                pool.wait_ge(kq_stored, 16 * 2 * STORES)
                pool.memset(hist[:, :, :, 0:RN], 0.0).then_inc(state, 1)
                pool.memset(hist[:, :, :, RN:RN + 1], 1.0).then_inc(state, 1)
                with pool.Fori(0, R_ITERS) as it:
                    for s in range(UNROLL):
                        for b in range(B):
                            at = s * 2 + b
                            g = slice(b * RG, (b + 1) * RG)
                            wait_apart(pool, (state, it * (2 * UNROLL) + (at + 1)))
                            bt = beta[:, bass.ds(it * UNROLL + s, 1), g].rearrange("p t g -> p (t g)")
                            pool.tensor_tensor(decay[:, b, :, :], hist[:, (s - 1) % UNROLL, g, 0:RN],
                                               bt.unsqueeze(2).broadcast_to([P, RG, RN]), ALU.mult).then_inc(decayed, 1)

            for ph in range(phases):
                if ph:
                    recurrence()
                for step in FIRST:
                    if step[0] == "rope":
                        rope(ph, 0, step[1], 0, first=True)
                with pool.Fori(0, layers) as l:
                    with pool.Fori(0, POS) as p:
                        i = l * POS + p
                        for step in ORDER:
                            if step[0] == "rope":
                                rope(ph, i + 1, step[1], 0)

        @block.tensor
        def _(pe):
            def ring_chunk(u, rb, c, emit):
                if not isinstance(rb, int) or rb + c >= 2:
                    pe.wait_ge(chunk_out, rb + (c - 1))
                emit(ring[(u + c) % 2]).then_inc(ring_full, 1)

            def turn(ph, i, b, rb, u, first=False):
                pe.wait_ge(rot_ready, nA(ph, i, b) + 1)
                for c in range(4):
                    def emit(bank):
                        for j in range(4):
                            at = (4 * c + j) * P
                            ins = pe.transpose(bank[:, j * P:(j + 1) * P], qk[:, b, at:at + P], ident[:, :])
                        return ins
                    ring_chunk(u, rb, c, emit)

            def score(ph, i, b, rb, u, first=False):
                wait_apart(pe, (chunk_out, rb_of(ph, i, ("turn", b)) + 4),
                           (s_read, nB(ph, i, b) + START))
                for k in range(PAIRS):
                    for w in range(P // WIN):
                        for e in range(2):
                            at = e * BANK + k * 2 * WIN
                            ins = pe.matmul(psS[w * WIN:(w + 1) * WIN, at:at + 2 * WIN],
                                            qT[e * DH:(e + 1) * DH, b, k, w * WIN:(w + 1) * WIN],
                                            kT[e * DH:(e + 1) * DH, b, k, w * WIN:(w + 2) * WIN],
                                            start=True, stop=True)
                ins.then_inc(s_done, 1)

            def load(ph, i1, b, rb, u, first=False):
                n = nA(ph, i1, b)
                pe.wait_ge(x_copied, n + 1)
                if first:
                    pe.wait_ge(x_done, X_BASE[ph] + SLOTS)
                else:
                    pe.wait_ge(x_done, i1 * 2 + (X_BASE[ph] + SLOTS - 4 + b + 1))
                pe.transpose(psM[b][:, 0:P], xcur[:, b, :], ident[:, :]).then_inc(x_turned, 1)

            def project(ph, i1, b, rb, u, chunks, col):
                pe.wait_ge(xs_ready, nA(ph, i1, b) + 1)
                pe.wait_ge(in_w, loads_of(ph, i1 // POS))
                for c in range(chunks):
                    at = col + c * BANK
                    ring_chunk(u, rb, c, lambda bank: pe.matmul(
                        bank[:, :], xs[:, b, 0:P], wqkv[:, bass.ds(par(i1), 1), at:at + BANK], start=True, stop=True))

            def qk_proj(ph, i1, b, rb, u, first=False):
                project(ph, i1, b, rb, u, 4, 0)

            def v_proj(ph, i1, b, rb, u, first=False):
                project(ph, i1, b, rb, u, 2, 2 * INNER)

            def pturn(ph, i, b, rb, u, first=False):
                pe.wait_ge(p_ready, nB(ph, i, b) + 1 + START)
                for c in range(4):
                    def emit(bank):
                        for j in range(4):
                            ins = pe.transpose(bank[:, j * P:(j + 1) * P], p_pad[:, 4 * c + j, :], ident[:, :])
                        return ins
                    ring_chunk(u, rb, c, emit)

            def psO_free(ph, i, step):
                pe.wait_ge(oT_ready, nB(ph, i, 0) + earlier("pv", step) + START)
                pe.wait_ge(gate_ready, nB(ph, i, 0) + earlier("up", step) + START)

            def pv(ph, i, b, rb, u, first=False):
                pe.wait_ge(chunk_out, rb_of(ph, i, ("pturn", b)) + 4)
                pe.wait_ge(v_edge, (nA(ph, i, b) + 1) * 16)
                pe.wait_ge(v_rest, (nA(ph, i, b) + 1) * 16)
                pe.wait_ge(ub_ready, i // POS + (layers * ph + 1))
                psO_free(ph, i, ("pv", b))
                o = psO[:, :].rearrange("p (k a w q) -> p k a w q", k=PAIRS, a=2, w=2)
                pr = pT[:, :, :].rearrange("p h (a w q) -> p h a w q", a=2, w=2)
                for k in range(PAIRS):
                    for odd, v in ((1, v_al), (0, v_sh)):
                        for e in range(2):
                            at = (2 * k + e) * DH
                            ins = pe.matmul(o[e * DH:(e + 1) * DH, k, :, odd, :], v[:, b, at:at + DH],
                                            pr[:, e * PAIRS + k, :, odd, :], start=True, stop=True)
                ins.then_inc(pv_done, 1)

            def out_proj(ph, i, b, rb, u, first=False):
                pe.wait_ge(oT_ready, nB(ph, i, b) + 1 + START)
                pe.wait_ge(xs_ready, nA(ph, i + 1, b) + 1)
                for k in range(PAIRS):
                    ins = pe.matmul(psM[b][:, 0:DIM], oT[:, k, :], wo[:, bass.ds(par(i), 1), k, :],
                                    start=(k == 0), stop=(k == PAIRS - 1))
                ins.then_inc(y_done, 1)

            def ln(ph, i, b, rb, u, first=False):
                pe.wait_ge(xmid_ready, nB(ph, i, b) + 1)
                pe.transpose(psM[b][:, 0:P], xmid[:, b, :], ident[:, :]).then_inc(m_turned, 1)

            def cent(ph, i, b, rb, u, first=False):
                pe.wait_ge(fs_ready, nB(ph, i, b) + 1 + START)
                pe.matmul(psM[b][:, 0:P], center[:, :], fs[:, b, 0:P], start=True, stop=True).then_inc(c_done, 1)

            def var(ph, i, b, rb, u, first=False):
                pe.wait_ge(c_ready, nB(ph, i, b) + 1)
                pe.matmul(psM[b][:, 0:1], csq[:, b, :], mean_col[:, :], start=True, stop=True).then_inc(var_done, 1)

            def up(ph, i, b, rb, u, first=False):
                psO_free(ph, i, ("up", b))
                for j in range(2):
                    ins = pe.matmul(psO[:, j * BANK:j * BANK + FF], cg[:, b, :],
                                    w1[:, bass.ds(par(i), 1), j * FF:(j + 1) * FF], start=True, stop=True)
                ins.then_inc(up_done, 1)

            def gturn(ph, i, b, rb, u, first=False):
                pe.wait_ge(g_ready, nB(ph, i, b) + 1)
                for j, (a, z) in enumerate(FF_CUTS):
                    ins = pe.transpose(psM[b][0:z - a, j * P:(j + 1) * P], ag[:, b, a:z], ident[:, :])
                ins.then_inc(g_turned, 1)

            def down(ph, i, b, rb, u, first=False):
                pe.wait_ge(gT_ready, nB(ph, i, b) + 1)
                for j, (a, z) in enumerate(FF_CUTS):
                    pe.matmul(psM[b][:, 0:DIM], gT[0:z - a, j, :], w2[0:z - a, bass.ds(par(i), 1), j, :],
                              start=(j == 0), stop=False)
                pe.matmul(psM[b][:, 0:DIM], ones[0:1, :], b2r[0:1, bass.ds(par(i), 1), :],
                          start=False, stop=True).then_inc(y2_done, 1)

            steps = {"turn": turn, "score": score, "load": load, "qk": qk_proj, "v": v_proj, "pturn": pturn,
                     "pv": pv, "wo": out_proj, "ln": ln, "cent": cent, "var": var, "up": up, "gturn": gturn,
                     "down": down}

            def rb_of(ph, i, step):
                return ring_base(ph, i) + RING_AT[step]

            def recurrence():
                ffn_over(pe)
                pe.wait_ge(in_r, 16 * R_DMAS)

                def piece(u, emit):
                    if u >= 2:
                        pe.wait_ge(piece_out, u - 1)
                    emit(ring[u % 2]).then_inc(piece_full, 1)

                def turned(srcs):
                    def emit(bank):
                        for j, src in enumerate(srcs):
                            ins = pe.transpose(bank[:, j * P:(j + 1) * P], src, ident[:, :])
                        return ins
                    return emit

                for n in range(N_PIECES[0]):
                    piece(n, turned([w_raw[:, j, :] for j in range(4 * n, min(4 * n + 4, 11))]))
                pe.wait_ge(x_done, X_N + SLOTS)
                for n in range(N_PIECES[1]):
                    piece(PIECE[1] + n, turned([x_tok[:, j, :] for j in range(4 * n, 4 * n + 4)]))
                pe.wait_ge(piece_out, PIECE[2])
                for n in range(N_PIECES[2]):
                    piece(PIECE[2] + n, lambda bank: pe.matmul(
                        bank[:, :], w_t[:, 0, :], xT[:, n * BANK:(n + 1) * BANK], start=True, stop=True))
                pe.wait_ge(piece_out, PIECE[3])
                for j, first in ((3, 5), (4, 7)):
                    for n in range(N_PIECES[j]):
                        g, c = n // (SLOTS // 4), n % (SLOTS // 4)
                        piece(PIECE[j] + n, lambda bank: pe.matmul(
                            bank[:, :], w_t[:, first + g, :], xpT[:, c * BANK:(c + 1) * BANK], start=True, stop=True))
                for n in range(N_PIECES[5]):
                    piece(PIECE[5] + n, lambda bank: pe.matmul(
                        bank[:, :], xpT[:, n * P:(n + 1) * P], w_t[:, 1:5, :].rearrange("p w m -> p (w m)"),
                        start=True, stop=True))

                def spread_block(a, it, hb, bank):
                    return pe.matmul(bank[:, :], spread[:, :],
                                     kq_in[:, bass.ds(it % 2, 1), a, hb * BCOLS:(hb + 1) * BCOLS],
                                     start=True, stop=True)

                pe.wait_ge(in_kq, 16)
                pe.wait_ge(piece_out, PIECE[6])
                spread_block(0, 0, 0, ring[0]).then_inc(k_spread, 1)
                spread_block(1, 0, 0, psM[1]).then_inc(q_spread, 1)
                spread_block(1, 0, 0, psM[0]).then_inc(q_spread, 1)
                with pe.Fori(0, R_ITERS) as it:
                    for hb in range(HALVES):
                        nxt, nb = (it, 1) if hb == 0 else (it + 1, 0)
                        pe.wait_ge(in_kq, nxt * 16 + 16)
                        pe.wait_ge(keys_ready, it * HALVES + hb + START)
                        spread_block(0, nxt, nb, ring[nb]).then_inc(k_spread, 1)
                        pe.wait_ge(q_used, it * HALVES + (hb + 1))
                        spread_block(1, nxt, nb, psM[nb]).then_inc(q_spread, 1)
                pe.wait_ge(cell, 1)
                for slot in range(SLOTS):
                    ps, b = slot // B, slot % B
                    bank = (psS, psO)[slot // (SLOTS // 2)]
                    at = slot % (SLOTS // 2) * DIM
                    for g in range(RG):
                        ins = pe.matmul(bank[:, at:at + DIM], sq[:, BLOCK + ps * P:BLOCK + (ps + 1) * P, b * RG + g],
                                        w_t[:, 9 + g, :], start=(g == 0), stop=(g == RG - 1))
                ins.then_inc(cell_y, 1)

            for signal in early[nc.tensor]:
                pe.sem_inc(signal, START)
            pe.wait_ge(consts, CONSTS)
            for ph in range(phases):
                if ph:
                    recurrence()
                for step in FIRST:
                    if step[0] in steps:
                        at = RING_AT0.get(step, 0)
                        steps[step[0]](ph, 0, step[1], R_N * ph + at, at, first=True)
                with pe.Fori(0, layers) as l:
                    pe.wait_ge(bb_ready, l + (layers * ph + 1))
                    pe.wait_ge(in_w, loads_of(ph, l))
                    pe.wait_ge(oT_ready, l * (2 * POS) + B_N * ph + START)
                    pe.wait_ge(gate_ready, l * (2 * POS) + B_N * ph + START)
                    for j in range(2):
                        half = bass.ds(l % 2, 1)
                        dst = psO[:, j * BANK:j * BANK + FF]
                        pe.matmul(dst, bbc[:, :], w1[:, half, j * FF:(j + 1) * FF], start=True, stop=False)
                        ins = pe.matmul(dst, ones[0:1, :], b1r[0:1, half, j * FF:(j + 1) * FF], start=False, stop=True)
                    ins.then_inc(ub_done, 1)
                    with pe.Fori(0, POS) as p:
                        i = l * POS + p
                        for step in ORDER:
                            if step[0] in steps:
                                at = RING_AT.get(step, 0)
                                i_of = i + 1 if step[0] in AHEAD else i
                                steps[step[0]](ph, i_of, step[1], ring_base(ph, i) + at, at)

        @block.scalar
        def _(act):
            def copy(dst, src, scale=1.0):
                return act.activation(dst, src, ACT.Copy, scale=scale)

            def carry_in(dst, b, p_at, sem_):
                copy(dst[DIM // 2:DIM, b, 0:1],
                     dst[DIM // 2:DIM, b, bass.ds((P + 1) - (p_at + POS - 1) // POS, 1)]).then_inc(sem_, 1)

            def shift_in(dst, b, bank, sem_):
                half = DIM // 2
                copy(dst[0:half, b, 0:P], bank[0:half, 0:P])
                copy(dst[half:DIM, b, 1:P + 1], bank[half:DIM, 0:P]).then_inc(sem_, 1)

            def load(ph, i1, b, rb, first=False):
                n = nA(ph, i1, b)
                act.wait_ge(x_done, i1 * 2 + (X_BASE[ph] + b + 1))
                if not (first and ph == 0):
                    act.wait_ge(x_turned, n - 1)
                copy(xcur[:, b, :], x_tok[:, bass.ds(slot_of(i1, b), 1), :]).then_inc(x_copied, 1)
                if not (first and ph == 0):
                    act.wait_ge(xs_ready, n - 1)
                carry_in(xs, b, i1 % POS, xs_carry)
                act.wait_ge(x_turned, n + 1)
                act.wait_ge(xs_carry, n + 1)
                shift_in(xs, b, psM[b], xs_ready)

            def qk_out(ph, i1, b, rb, first=False):
                n = nA(ph, i1, b)
                if not (first and ph == 0):
                    act.wait_ge(rot_ready, n - 1)
                for c in range(4):
                    at, bank = c * BANK, ring[(rb_par(rb) + c) % 2]
                    act.wait_ge(ring_full, rb[0] + (c + 1))
                    copy(qk[:, b, at:at + BANK], bank[:, :])
                    act.activation(scr[:, b, at:at + BANK], bank[:, :], ACT.Square).then_inc(chunk_out, 1)

            def rb_par(rb):
                return rb[1]

            def v_out(ph, i1, b, rb, first=False):
                act.wait_ge(v_edge, (nA(ph, i1, b) + 1) * 16)
                for c in range(2):
                    act.wait_ge(ring_full, rb[0] + (c + 1))
                    copy(v_al[:, b, c * BANK:(c + 1) * BANK], ring[(rb[1] + c) % 2][:, :]).then_inc(chunk_out, 1)

            def turn(ph, i, b, rb, first=False):
                copy(kT[:, b, :, 0:WIN],
                     kT[:, b, :, bass.ds((P + WIN) - ((i % POS + POS - 1) // POS) * WIN, WIN)]).then_inc(tail_copied, 1)
                act.wait_ge(tail_copied, nB(ph, i, b) + 1)
                for c in range(4):
                    act.wait_ge(ring_full, rb[0] + (c + 1))
                    src = ring[(rb[1] + c) % 2][:, :].rearrange("p (j t) -> p j t", t=P)
                    k = 4 * (c % 2)
                    dst = qT[:, b, k:k + 4, :] if c < 2 else kT[:, b, k:k + 4, WIN:WIN + P]
                    copy(dst, src).then_inc(chunk_out, 1)

            def soft(ph, i, b, rb, first=False):
                act.wait_ge(sub_done, nB(ph, i, b) + 1)
                act.activation(sm[:, :, :], sm[:, :, :], ACT.Exp).then_inc(exp_done, 1)

            def pturn(ph, i, b, rb, first=False):
                for c in range(4):
                    act.wait_ge(ring_full, rb[0] + (c + 1))
                    src = ring[(rb[1] + c) % 2][:, :].rearrange("p (j t) -> p j t", t=P)
                    copy(pT[:, 4 * c:4 * c + 4, :], src).then_inc(chunk_out, 1)

            def pv(ph, i, b, rb, first=False):
                act.wait_ge(pv_done, nB(ph, i, b) + 1)
                act.wait_ge(y_done, nB(ph, i, b) + START)
                copy(oT[:, :, :], psO[:, :].rearrange("p (k t) -> p k t", t=P)).then_inc(oT_ready, 1)

            def ln(ph, i, b, rb, first=False):
                n = nB(ph, i, b)
                act.wait_ge(fs_ready, n + START)
                carry_in(fs, b, i % POS, fs_carry)
                act.wait_ge(m_turned, n + 1)
                act.wait_ge(fs_carry, n + 1)
                shift_in(fs, b, psM[b], fs_ready)

            def cent(ph, i, b, rb, first=False):
                act.wait_ge(c_done, nB(ph, i, b) + 1)
                act.activation(csq[:, b, :], psM[b][:, 0:P], ACT.Square)
                copy(cg[:, b, :], psM[b][:, 0:P], gcol[:, bass.ds(i // POS, 1)]).then_inc(c_ready, 1)

            def up(ph, i, b, rb, first=False):
                act.wait_ge(gate_ready, nB(ph, i, b) + 1 + START)
                act.activation(ag[:, b, FF:2 * FF], ag[:, b, FF:2 * FF], ACT.Gelu).then_inc(gelu_done, 1)

            def gturn(ph, i, b, rb, first=False):
                act.wait_ge(g_turned, nB(ph, i, b) + 1)
                act.wait_ge(y2_done, nB(ph, i, 0) + earlier("down", ("gturn", b)) + START)
                last = FF_CUTS[-1][1] - FF_CUTS[-1][0]
                copy(gT[:, 0:2, :], psM[b][:, 0:2 * P].rearrange("p (j t) -> p j t", t=P))
                copy(gT[0:last, 2, :], psM[b][0:last, 2 * P:3 * P]).then_inc(gT_ready, 1)

            steps = {"load": load, "qk": qk_out, "v": v_out, "turn": turn, "soft": soft, "pturn": pturn, "pv": pv,
                     "ln": ln, "cent": cent, "up": up, "gturn": gturn}

            def recurrence():
                ffn_over(act)

                def piece(u):
                    act.wait_ge(piece_full, u + 1)
                    return ring[u % 2]

                for n in range(N_PIECES[0]):
                    k = min(4, 11 - 4 * n)
                    copy(w_t[:, 4 * n:4 * n + k, :], piece(n)[:, 0:k * P].rearrange("p (w m) -> p w m", m=P)
                         ).then_inc(piece_out, 1)
                for n in range(N_PIECES[1]):
                    copy(xT[:, n * BANK:(n + 1) * BANK], piece(PIECE[1] + n)[:, :]).then_inc(piece_out, 1)
                for n in range(N_PIECES[2]):
                    act.activation(xpT[:, n * BANK:(n + 1) * BANK], piece(PIECE[2] + n)[:, :], ACT.Silu
                                   ).then_inc(piece_out, 1)
                for j, dst in ((3, v_neg), (4, beta)):
                    for n in range(N_PIECES[j]):
                        g, c = n // (SLOTS // 4), n % (SLOTS // 4)
                        bank = piece(PIECE[j] + n)[:, :].rearrange("p (s b t) -> p s b t", b=B, t=P)
                        d = dst[:, c * (BANK // B):(c + 1) * (BANK // B), g::RG].rearrange("p (s t) b -> p s b t", t=P)
                        if j == 3:
                            ins = copy(d, bank, -1.0)
                        else:
                            ins = act.activation(d, bank, ACT.Sigmoid, bias=beta_bias[:, g:g + 1])
                        ins.then_inc(piece_out, 1)
                for n in range(N_PIECES[5]):
                    if n == SLOTS // 2:
                        act.wait_ge(kq_stored, 16 * STORES)
                    copy(kq[:, n % (SLOTS // 2), :, :], piece(PIECE[5] + n)[:, :].rearrange("p (a m) -> p a m", a=2)
                         ).then_inc(piece_out, 1)

                def keys_out(n_of, it, hb, first=False):
                    act.wait_ge(k_spread, n_of + 1)
                    if not first:
                        act.wait_ge(arg_ready, (n_of - 1) * (2 * BLOCK) + START)
                    ks = slice(hb * BLOCK, (hb + 1) * BLOCK)
                    copy(keys[:, ks, :, 0:RN].rearrange("p t g j -> p (t g) j"), ring[hb][:, :].rearrange("p (n j) -> p n j", j=RN))
                    copy(keys[:, ks, :, RN],
                         v_neg[:, bass.ds(it * UNROLL + hb * BLOCK, BLOCK), :]).then_inc(keys_ready, 1)

                act.wait_ge(state, 2)
                keys_out(0, 0, 0, first=True)
                with act.Fori(0, R_ITERS) as it:
                    for hb in range(HALVES):
                        if hb == 0:
                            keys_out(it * HALVES + 1, it, 1)
                        else:
                            keys_out(it * HALVES + 2, (it + 1) % R_ITERS, 0)
                        for s in range(hb * BLOCK, (hb + 1) * BLOCK):
                            for b in range(B):
                                act.wait_ge(arg_ready, it * (2 * UNROLL) + (2 * s + b + 1) + START)
                                act.activation(hist[:, s, b * RG:(b + 1) * RG, 0:RN], arg[:, b, :, :], ACT.Tanh
                                               ).then_inc(state, 1)
                act.wait_ge(sq_ready, R_ITERS * HALVES + 1 + START)
                act.wait_ge(q_spread, R_ITERS * HALVES + 2)
                act.wait_ge(in_kq, 16 * (R_ITERS + 1))
                act.activation(gate, sq[:, BLOCK:, :], ACT.Sigmoid).then_inc(gate_r, 1)

            for signal in early[nc.scalar]:
                act.sem_inc(signal, START)
            act.wait_ge(consts, CONSTS)
            for ph in range(phases):
                if ph:
                    recurrence()
                for step in FIRST:
                    if step[0] in steps:
                        at = RING_AT0.get(step, 0)
                        steps[step[0]](ph, 0, step[1], (R_N * ph + at, at), first=True)
                with act.Fori(0, layers) as l:
                    act.wait_ge(ub_done, l + layers * ph + START)
                    act.activation(bbc[:, :], ones[:, :], ACT.Copy, scale=bcol[:, bass.ds(l, 1)]).then_inc(bb_ready, 1)
                    act.wait_ge(ub_done, l + (layers * ph + 1) + START)
                    act.wait_ge(gate_ready, l * (2 * POS) + B_N * ph + START)
                    copy(up_bias[:, :].rearrange("p (j f) -> p j f", j=2),
                         psO[:, :].rearrange("p (j f) -> p j f", j=2)[:, :, 0:FF]).then_inc(ub_ready, 1)
                    with act.Fori(0, POS) as p:
                        i = l * POS + p
                        for step in ORDER:
                            if step[0] in steps:
                                at = RING_AT.get(step, 0)
                                i_of = i + 1 if step[0] in AHEAD else i
                                steps[step[0]](ph, i_of, step[1], (ring_base(ph, i) + at, at))

        @block.vector
        def _(dv):
            chain = [0, 0]
            chain_sem = [dve]

            def link(ins):
                chain[1] += 1
                ins.then_inc(chain_sem[0], 1)
                dv.wait_ge(chain_sem[0], chain[0] + chain[1])

            def rsqrt(dst, src, n, nt=nt):
                y, t, h = nt[:, 0, 0:n], nt[:, 1, 0:n], nt[:, 2, 0:n]
                link(dv.tensor_scalar(t.bitcast(U32), src.bitcast(U32), 1, None, ALU.logical_shift_right))
                link(dv.tensor_scalar(y.bitcast(I32), t.bitcast(I32), -1.0, RSQRT_MAGIC, ALU.mult, ALU.add))
                link(dv.tensor_scalar(h, src, -0.5, None, ALU.mult))
                for r in range(3):
                    link(dv.tensor_tensor(t, y, y, ALU.mult))
                    link(dv.tensor_tensor(t, t, h, ALU.mult))
                    link(dv.scalar_tensor_tensor(out=dst if r == 2 else y, in0=t, scalar=1.5, in1=y,
                                                 op0=ALU.add, op1=ALU.mult))

            def norm(ph, i1, b, rb, first=False):
                for c in range(4):
                    dv.wait_ge(chunk_out, rb + (c + 1))
                    ins = dv.tensor_reduce(ss[:, b, 8 * c:8 * c + 8],
                                           scr[:, b, c * BANK:(c + 1) * BANK].rearrange("p (h d) -> p h d", d=DH),
                                           AX_X, ALU.add)
                    link(ins)
                link(dv.tensor_scalar(ss[:, b, :], ss[:, b, :], 1e-24, None, ALU.max))
                rsqrt(ss[:, b, :], ss[:, b, :], 2 * HEADS)
                q = qk[:, b, :].rearrange("p (h d) -> p h d", d=DH)
                dv.tensor_tensor(q, q, ss[:, b, :].unsqueeze(2).broadcast_to([P, 2 * HEADS, DH]),
                                 ALU.mult).then_inc(qn_ready, 1)

            def rope(ph, i1, b, rb, first=False):
                n = nA(ph, i1, b)
                dv.wait_ge(rt_ready, i1 + ((ITERS + 1) * ph + 1))
                dv.wait_ge(qn_ready, n + 1)
                for t in range(2):
                    tab = rope_tab[:, bass.ds(i1 % 2, 1), t, :].broadcast_to([P, HEADS, DH])
                    cols = slice(t * INNER, (t + 1) * INNER)
                    ins = dv.tensor_tensor(scr[:, b, cols].rearrange("p (h d) -> p h d", d=DH),
                                           qk[:, b, cols].rearrange("p (h d) -> p h d", d=DH), tab, ALU.mult)
                link(ins)
                dv.wait_ge(rs_ready, (n + 1) * 4)
                dv.tensor_tensor(qk[:, b, :], scr[:, b, :], rot[:, :], ALU.add).then_inc(rot_ready, 1)

            def soft(ph, i, b, rb, first=False):
                n = nB(ph, i, b)
                dv.wait_ge(s_done, n + 1)
                dv.wait_ge(p_ready, n + START)
                hd = sm[:, :, :]
                dv.tensor_tensor(hd, psS[:, :].rearrange("p (h j) -> p h j", j=2 * WIN),
                                 masks[:, bass.ds((i % POS + POS - 1) // POS, 1), :].broadcast_to([P, HEADS, 2 * WIN]),
                                 ALU.add).then_inc(s_read, 1)
                dv.wait_ge(s_read, n + 1 + START)
                link(dv.tensor_reduce(mx[:, :], hd, AX_X, ALU.max))
                dv.tensor_tensor(hd, hd, mx[:, :].unsqueeze(2).broadcast_to([P, HEADS, 2 * WIN]),
                                 ALU.subtract).then_inc(sub_done, 1)
                dv.wait_ge(exp_done, n + 1)
                link(dv.tensor_reduce(rl[:, :], hd, AX_X, ALU.add))
                link(dv.reciprocal(rl[:, :], rl[:, :]))
                if b == 0:
                    dv.wait_ge(ring_full, ring_base(ph, i) + (RING_AT["pturn", 1] + 4 - RING_N))
                else:
                    dv.wait_ge(ring_full, ring_base(ph, i) + (RING_AT["pturn", 0] + 4))
                half = P // 2
                for a, z in ((0, half), (half, P)):
                    ins = dv.tensor_tensor(p_pad[a:z, :, a:z], sm[a:z, :, :],
                                           rl[a:z, :].unsqueeze(2).broadcast_to([half, HEADS, half]), ALU.mult)
                ins.then_inc(p_ready, 1)

            def out_proj(ph, i, b, rb, first=False):
                dv.wait_ge(y_done, nB(ph, i, b) + 1 + START)
                dv.tensor_tensor(xmid[:, b, :], psM[b][:, 0:DIM], x_tok[:, bass.ds(slot_of(i, b), 1), :].squeeze(1),
                                 ALU.add).then_inc(xmid_ready, 1)

            def var(ph, i, b, rb, first=False):
                dv.wait_ge(var_done, nB(ph, i, b) + 1)
                link(dv.tensor_scalar(rstd[:, b:b + 1], psM[b][:, 0:1], LN_EPS, None, ALU.add))
                rsqrt(rstd[:, b:b + 1], rstd[:, b:b + 1], 1)

            def up(ph, i, b, rb, first=False):
                n = nB(ph, i, b)
                dv.wait_ge(up_done, n + 1)
                for j in range(2):
                    ins = dv.scalar_tensor_tensor(out=ag[:, b, j * FF:(j + 1) * FF], in0=psO[:, j * BANK:j * BANK + FF],
                                                  scalar=rstd[:, b:b + 1], in1=up_bias[:, j * FF:(j + 1) * FF],
                                                  op0=ALU.mult, op1=ALU.add)
                ins.then_inc(gate_ready, 1)

            def gturn(ph, i, b, rb, first=False):
                dv.wait_ge(gelu_done, nB(ph, i, b) + 1)
                dv.tensor_tensor(ag[:, b, 0:FF], ag[:, b, 0:FF], ag[:, b, FF:2 * FF], ALU.mult).then_inc(g_ready, 1)

            def down(ph, i, b, rb, first=False):
                dv.wait_ge(y2_done, nB(ph, i, b) + 1 + START)
                dv.tensor_tensor(x_tok[:, bass.ds(slot_of(i, b), 1), :].squeeze(1), psM[b][:, 0:DIM], xmid[:, b, :],
                                 ALU.add).then_inc(x_done, 1)

            steps = {"norm": norm, "rope": rope, "soft": soft, "wo": out_proj, "var": var, "up": up,
                     "gturn": gturn, "down": down}

            def run(step, ph, i, rb, base, first=False):
                chain[0], chain[1] = base, 0
                steps[step[0]](ph, i, step[1], rb, first)
                assert chain[1] == LINKS.get(step[0], 0), (step, chain[1])

            def layernorm(ph, base):
                chain[0], chain[1] = base, 0
                for s in range(SLOTS):
                    ins = dv.bn_stats(stats[:, s, :], x_in[:, s, :])
                link(ins)
                for s in range(SLOTS):
                    ins = dv.bn_aggr(mv[:, s, :], stats[:, s, :])
                link(ins)
                link(dv.tensor_scalar(rs16[:, :], mv[:, :, 1], LN_EPS, None, ALU.add))
                rsqrt(rs16[:, :], rs16[:, :], SLOTS)
                for s in range(SLOTS):
                    dv.tensor_scalar(x_tok[:, s, :], x_in[:, s, :], mv[:, s, 0:1], rs16[:, s:s + 1],
                                     ALU.subtract, ALU.mult).then_inc(x_done, 1)

            def recurrence():
                ffn_over(dv)
                layernorm(0, D_N)
                chain[0], chain[1], chain_sem[0] = 0, 0, rdve
                rows = SLOTS // 2 * RH
                for hf in range(2):
                    dv.wait_ge(piece_out, PIECE[5] + (hf + 1) * (SLOTS // 2))
                    k = kq[:, :, 0, :]
                    link(dv.tensor_tensor(ksq, k, k, ALU.mult))
                    link(dv.tensor_reduce(knorm, ksq.rearrange("p s (h j) -> p (s h) j", j=RN), AX_X, ALU.add))
                    rsqrt(ksq[:, 0, 0:rows], knorm, rows, nt_r)
                    link(dv.tensor_tensor(knorm, knorm, ksq[:, 0, 0:rows], ALU.mult))
                    link(dv.tensor_scalar(knorm, knorm, 1e-6, None, ALU.add))
                    link(dv.reciprocal(knorm, knorm))
                    for n in range(SLOTS // 2):
                        kn = k[:, n, :].rearrange("p (h j) -> p h j", j=RN)
                        ins = dv.tensor_tensor(kn, kn, knorm[:, n * RH:(n + 1) * RH].unsqueeze(2).broadcast_to([P, RH, RN]),
                                               ALU.mult)
                    ins.then_inc(kn_ready, 1)
                base = chain[1]
                dv.wait_ge(kq_stored, 16 * 2 * STORES)

                def query(n_of, hb):
                    ks = slice((1 - hb) * BLOCK, (2 - hb) * BLOCK)
                    dv.wait_ge(q_spread, n_of + 1)
                    dv.tensor_tensor(qprod, hist[:, ks, :, 0:RN].rearrange("p t g j -> p (t g) j"),
                                     psM[1 - hb][:, :].rearrange("p (n j) -> p n j", j=RN), ALU.mult).then_inc(q_used, 1)
                    dv.wait_ge(q_used, n_of + 1)
                    dv.tensor_reduce(sq[:, bass.ds(n_of * BLOCK, BLOCK), :].rearrange("p t g -> p (t g)"),
                                     qprod, AX_X, ALU.add).then_inc(sq_ready, 1)

                per = 6
                with dv.Fori(0, R_ITERS) as it:
                    for s in range(UNROLL):
                        hb, at = s // BLOCK, it * (per * UNROLL) + (base + per * s)
                        if s % BLOCK == 0:
                            dv.wait_ge(keys_ready, it * HALVES + (hb + 1) + START)
                        pairs = [(b, slice(b * RG, (b + 1) * RG)) for b in range(B)]
                        for b, g in pairs:
                            dv.wait_ge(state, it * (2 * UNROLL) + (2 * s + b + 1))
                            dv.tensor_tensor(prod[:, b, :, :], hist[:, (s - 1) % UNROLL, g, :], keys[:, s, g, :],
                                             ALU.mult).then_inc(rdve, 1)
                        for b, g in pairs:
                            dv.wait_ge(rdve, at + (b + 1))
                            dv.tensor_reduce(nd[:, b, :], prod[:, b, :, :], AX_X, ALU.add).then_inc(rdve, 1)
                        for b, g in pairs:
                            dv.wait_ge(rdve, at + (b + 3))
                            dv.tensor_tensor(upd[:, b, :, :], keys[:, s, g, 0:RN],
                                             nd[:, b, :].unsqueeze(2).broadcast_to([P, RG, RN]), ALU.mult).then_inc(rdve, 1)
                        for b, g in pairs:
                            dv.wait_ge(rdve, at + (b + 5))
                            dv.wait_ge(decayed, it * (2 * UNROLL) + (2 * s + b + 1))
                            dv.tensor_tensor(arg[:, b, :, :], decay[:, b, :, :], upd[:, b, :, :],
                                             ALU.subtract).then_inc(arg_ready, 1)
                        if s % BLOCK == 0:
                            dv.wait_ge(sq_ready, it * HALVES + hb + START)
                            query(it * HALVES + hb, hb)
                dv.wait_ge(state, 2 * T + 2)
                dv.wait_ge(sq_ready, R_ITERS * HALVES + START)
                query(R_ITERS * HALVES, 0)
                dv.wait_ge(sq_ready, R_ITERS * HALVES + 1 + START)
                chain[0], chain[1] = base + per * T, 0
                g1, s1 = gate.rearrange("p t g -> p (t g)"), sq[:, BLOCK:, :].rearrange("p t g -> p (t g)")
                dv.wait_ge(gate_r, 1)
                link(dv.tensor_tensor(g1, g1, s1, ALU.mult))
                dv.tensor_tensor(s1, g1, s1, ALU.mult).then_inc(cell, 1)
                dv.wait_ge(cell_y, 1)
                for n, bank in enumerate((psS, psO)):
                    xi = x_in[:, n * (SLOTS // 2):(n + 1) * (SLOTS // 2), :].rearrange("p s d -> p (s d)")
                    ins = dv.tensor_tensor(xi, xi, bank[:, :], ALU.add)
                chain_sem[0], chain[0], chain[1] = fin, 1, 0
                link(ins)
                chain_sem[0] = dve

            for signal in early[nc.vector]:
                dv.sem_inc(signal, START)
            dv.wait_ge(in_x, 16 * B)
            for ph in range(phases):
                if ph:
                    recurrence()
                layernorm(ph, D_BASE[ph])
                base0 = D_BASE[ph] + LN_LINKS
                for step in FIRST:
                    if step[0] in steps:
                        rb = R_N * ph + RING_AT0.get(("qk", step[1]), 0)
                        run(step, ph, 0, rb, base0 + links_at0[step], first=True)
                with dv.Fori(0, layers) as l:
                    with dv.Fori(0, POS) as p:
                        i = l * POS + p
                        for step in ORDER:
                            if step[0] in steps:
                                i_of = i + 1 if step[0] in AHEAD else i
                                rb = ring_base(ph, i) + RING_AT.get(("qk", step[1]), 0)
                                run(step, ph, i_of, rb, i * links_n + (base0 + links_n0 + links_at[step]))
                dv.wait_ge(x_done, X_BASE[ph] + X_N)
                dv.scalar_tensor_tensor(out=x_in[:, :, :].rearrange("p s d -> p (s d)"),
                                        in0=x_tok[:, :, :].rearrange("p s d -> p (s d)"), scalar=0.5,
                                        in1=x_in[:, :, :].rearrange("p s d -> p (s d)"),
                                        op0=ALU.mult, op1=ALU.add).then_inc(fin, 1)
                dv.wait_ge(fin, 2 * ph + 1)


def rope_tables(n):
    half = np.arange(0, DH, 2, dtype=np.float32)
    inv_freq = (np.float32(1.0) / np.power(np.float32(10000.0), half / np.float32(DH))).astype(np.float32)
    t = np.arange(n, dtype=np.float32)
    freqs = t[:, None] * inv_freq[None, :]
    freqs = np.concatenate([freqs, freqs], -1)
    base = (half + np.float32(0.4 * DH)) / np.float32(1.4 * DH)
    power = (t - np.float32(n // 2)) / np.float32(WIN // 2)
    scale = np.power(base[None, :], power[:, None])
    scale = np.concatenate([scale, scale], -1)
    cos, sin = np.cos(freqs), np.sin(freqs)
    sin = sin * np.where(np.arange(DH) < DH // 2, np.float32(-1), np.float32(1))[None, :]
    qk_scale = np.float32(8.0)
    tabs = np.stack([qk_scale * cos * scale, cos / scale, qk_scale * sin * scale, sin / scale], 1)
    return np.ascontiguousarray(tabs.reshape(n // P, P, 4, DH).transpose(1, 0, 2, 3)).astype(np.float32)


def window_masks():
    q = np.arange(P)
    c = np.arange(2 * WIN)[None, :]
    far = (c > (q % WIN)[:, None] + WIN) | (c < (q % WIN)[:, None])
    edge = far | ((q < WIN)[:, None] & (c < WIN))
    return (np.stack([edge, far], 1) * -np.finfo(np.float32).max).astype(np.float32)


def spread_matrix():
    return np.repeat(np.eye(P // RN, dtype=np.float32), RN, axis=1)


def kernel(**inputs):
    import concourse.bacc as bacc
    from concourse.bass_utils import run_bass_kernel_spmd

    arrays = {n: np.ascontiguousarray(inputs["L0_" + n]) for n in (
        "attn_x", "attn_W_in", "attn_W_k", "attn_W_v", "attn_W_q", "attn_W_beta", "attn_b_beta", "attn_W_out",
        "ffn_Wqkv", "ffn_q_scale", "ffn_k_scale", "ffn_Wo", "ffn_ln_g", "ffn_ln_b", "ffn_W1", "ffn_b1", "ffn_W2",
        "ffn_b2")}
    shape = arrays["attn_x"].shape
    arrays["tables"] = rope_tables(shape[1])
    arrays["mask"] = window_masks()
    arrays["ident_in"] = np.eye(P, dtype=np.float32)
    arrays["spread_in"] = spread_matrix()
    nc = bacc.Bacc("TRN2", target_bir_lowering=False, num_devices=1)
    aps = {n.removeprefix("attn_").removeprefix("ffn_"):
           nc.dram_tensor(f"in_{n}", a.shape, mybir.dt.from_np(a.dtype), kind="ExternalInput").ap()
           for n, a in arrays.items()}
    out = nc.dram_tensor("out_x", shape, F32, kind="ExternalOutput").ap()
    build(nc, out=out, **aps)
    r = run_bass_kernel_spmd(nc, [{f"in_{n}": a for n, a in arrays.items()}], core_ids=[0])
    return r.results[0]["out_x"]
```

```python
from contextlib import ExitStack
from functools import partial

import numpy as np

import concourse.bass as bass
from concourse import mybir

F32 = mybir.dt.float32
I32 = mybir.dt.int32
U32 = mybir.dt.uint32
ALU = mybir.AluOpType
ACT = mybir.ActivationFunctionType
AX_X = mybir.AxisListType.X

P = 128
DIM = 128
LAYERS = 6
HEADS, DH = 16, 64
WIN = 32
INNER = HEADS * DH
PAIRS = HEADS // 2
FF = int(DIM * 4 * 2 / 3)
RH, RN = 8, 32
RG = RH * RN // P
UNROLL, BLOCK = 8, 4
FF_CUTS = [(0, 128), (128, 256), (256, FF)]
LN_EPS = 1e-5
BANK = 512
RSQRT_MAGIC = float(0x5F3759DF)

ORDER = [("turnk", 0), ("turnq", 0), ("scorea", 0), ("scoreb", 0), ("cosine", 1), ("rope", 1), ("load", 0),
         ("turnq", 1), ("turnk", 1), ("mask", 0), ("q", 0), ("prob", 0), ("scorea", 1), ("scoreb", 1),
         ("load", 1), ("pturna", 0), ("pturnb", 0), ("mask", 1), ("pva", 0), ("prob", 1), ("pvb", 0),
         ("k", 0), ("sumsq", 0), ("q", 1), ("wo", 0), ("norm", 0), ("pturna", 1), ("ln", 0), ("k", 1),
         ("pturnb", 1), ("cent", 0), ("sumsq", 1), ("pva", 1), ("cosine", 0), ("var", 0), ("pvb", 1),
         ("up", 0), ("wo", 1), ("gate", 0), ("v", 0), ("ln", 1), ("norm", 1), ("cent", 1), ("var", 1),
         ("gturn", 0), ("up", 1), ("gate", 1), ("down", 0), ("rope", 0), ("v", 1), ("gturn", 1),
         ("down", 1)]
AHEAD = ("load", "q", "k", "sumsq", "norm", "cosine", "rope", "v")
LATE = (("cosine", 1), ("rope", 1))
RING_USES = {"turnq": 2, "turnk": 2, "q": 2, "k": 2, "pturna": 2, "pturnb": 2, "v": 2}


def ring_offsets(order):
    at, out = 0, {}
    for name, b in order:
        if name in RING_USES:
            out[name, b] = at
            at += RING_USES[name]
    return out, at


def ahead(step):
    return step[0] in AHEAD and step not in LATE


FIRST = [s for s in ORDER if ahead(s)]
RING_AT, RING_N = ring_offsets(ORDER)
RING_AT0, RING_N0 = ring_offsets(FIRST)


ARENA = 23360


def build(nc, x, tables, mask, ident_in, spread_in, W_in, W_k, W_v, W_q, W_beta, b_beta, W_out,
          Wqkv, q_scale, k_scale, Wo, ln_g, ln_b, W1, b1, W2, b2, out, layers=LAYERS, phases=2):
    B, T, _ = x.shape
    POS = T // P
    SLOTS = POS * B
    ITERS = layers * POS
    A_N, B_N = 2 * (ITERS + 1), 2 * ITERS
    C_N = 2 * ITERS + 1
    X_N = SLOTS + B_N
    X_BASE = [0, X_N + SLOTS]
    R_N = RING_N0 + RING_N * ITERS

    with ExitStack() as ctx:
        def sb(name, shape, dt=F32):
            return ctx.enter_context(nc.sbuf_tensor(name, shape, dt))

        def sem(name):
            return ctx.enter_context(nc.semaphore(name))

        arena = sb("arena", [P, ARENA])

        def carver(start=0):
            at = [start]

            def cut(shape):
                n = int(np.prod(shape[1:]))
                a, at[0] = at[0], at[0] + n
                assert at[0] <= ARENA, at[0]
                v = arena[0:shape[0], a:a + n]
                if len(shape) == 2:
                    return v
                names = "abcde"[:len(shape) - 1]
                return v.rearrange(f"p ({' '.join(names)}) -> p {' '.join(names)}",
                                   **dict(zip(names[1:], shape[2:])))
            cut.at = at
            return cut

        ffn, rec = carver(), carver()
        x_in = sb("x_in", [P, SLOTS, DIM])
        x_tok = sb("x_tok", [P, SLOTS, DIM])
        wqkv = sb("wqkv", [DIM, 2, 3 * INNER])
        wo = sb("wo", [P, 2, PAIRS, DIM])
        w1 = sb("w1", [DIM, 2, 2 * FF])
        w2 = sb("w2", [P, 2, 3, DIM])
        b1r = sb("b1r", [1, 2, 2 * FF])
        b2r = sb("b2r", [1, 2, DIM])
        scales = sb("scales", [P, 2, 4, DH])
        rope_base = sb("rope_base", [P, POS, 4, DH])
        rope_tab = sb("rope_tab", [P, 2, 4, DH])
        masks = sb("masks", [P, 2, 2 * WIN])
        gcol = sb("gcol", [DIM, layers])
        bcol = sb("bcol", [DIM, layers])
        ident = sb("ident", [P, P])
        center = sb("center", [P, P])
        ones = sb("ones", [P, P])
        mean_col = sb("mean_col", [P, 1])
        bbc = sb("bbc", [P, P])
        up_bias = sb("up_bias", [P, 2 * FF])
        xcur = ffn([P, 2, DIM])
        xs = sb("xs", [P, 2, P + 2])
        fs = sb("fs", [P, 2, P + 2])
        qk = ffn([P, 2, 2 * INNER])
        scr = ffn([P, 2, 2 * INNER])
        rot = ffn([P, 2 * INNER])
        ss = ffn([P, 2, 2 * HEADS])
        qT = ffn([P, 2, PAIRS, P])
        kT = sb("kT", [P, 2, PAIRS, WIN + P + WIN])
        v_al = ffn([P, 2, INNER])
        v_sh = ffn([P, 2, INNER])
        sm = ffn([P, 2 * PAIRS, 2 * WIN])
        mx = ffn([P, HEADS])
        rl = ffn([P, HEADS])
        p_pad = sb("p_pad", [P, HEADS, P])
        pT = ffn([P, HEADS, P])
        oT = ffn([P, PAIRS, P])
        xmid = ffn([P, 2, DIM])
        cg = ffn([P, 2, P])
        csq = ffn([P, 2, P])
        rstd = ffn([P, 2])
        ag = ffn([P, 2, 2 * FF])
        gT = ffn([P, 3, P])
        nt = sb("nt", [P, 3, 2 * HEADS])
        stats = sb("stats", [P, SLOTS, 6])
        mv = sb("mv", [P, SLOTS, 2])
        rs16 = sb("rs16", [P, SLOTS])

        GR = B * RG
        w_t = rec([P, 11, P])
        v_neg = rec([P, T, GR])
        beta = rec([P, T, GR])
        beta_bias = rec([P, RG])
        spread = rec([4, P])
        prep, loop = carver(rec.at[0]), carver(rec.at[0])
        w_raw = prep([P, 11, P])
        xT = prep([P, SLOTS * P])
        xpT = prep([P, SLOTS * P])
        kq = prep([P, SLOTS // 2, 2, RH * RN])
        ksq = prep([P, SLOTS // 2, RH * RN])
        knorm = prep([P, SLOTS // 2 * RH])
        nt_r = prep([P, 3, SLOTS // 2 * RH])
        kq_in = loop([4, 2, 2, UNROLL * GR * RN])
        SQ_0 = BLOCK + 2
        sq = loop([P, SQ_0 + T, GR])
        keys = loop([P, UNROLL, GR, RN + 1])
        hist = loop([P, UNROLL, GR, RN + 1])
        prod = loop([P, B, RG, RN + 1])
        nd = loop([P, B, RG])
        upd = loop([P, B, RG, RN])
        decay = loop([P, B, RG, RN])
        arg = loop([P, B, RG, RN])
        queries = loop([P, 2, GR, RN])
        qprod = loop([P, 2, GR, RN])
        gate = carver(rec.at[0])([P, T, GR])

        ring = [ctx.enter_context(nc.psum_tensor(f"ring{j}", [P, BANK], F32)) for j in range(2)]
        psS = ctx.enter_context(nc.psum_tensor("psS", [P, 2 * BANK], F32))
        psO = ctx.enter_context(nc.psum_tensor("psO", [P, 2 * BANK], F32))
        psM = [ctx.enter_context(nc.psum_tensor(f"psM{j}", [P, BANK], F32)) for j in range(2)]

        in_x = sem("in_x")
        in_const = sem("in_const")
        in_w = sem("in_w")
        consts = sem("consts")
        x_done = sem("x_done")
        dve = sem("dve")
        x_copied = sem("x_copied")
        x_turned = sem("x_turned")
        xs_ready = sem("xs_ready")
        xs_carry = sem("xs_carry")
        fs_carry = sem("fs_carry")
        ring_full = sem("ring_full")
        chunk_out = sem("chunk_out")
        qn_ready = sem("qn_ready")
        rt_ready = sem("rt_ready")
        rs_ready = sem("rs_ready")
        rot_ready = sem("rot_ready")
        tail_copied = sem("tail_copied")
        s_done = sem("s_done")
        s_read = sem("s_read")
        sub_done = sem("sub_done")
        exp_done = sem("exp_done")
        p_ready = sem("p_ready")
        pv_done = sem("pv_done")
        oT_ready = sem("oT_ready")
        v_edge = sem("v_edge")
        v_rest = sem("v_rest")
        y_done = sem("y_done")
        xmid_ready = sem("xmid_ready")
        m_turned = sem("m_turned")
        fs_ready = sem("fs_ready")
        c_done = sem("c_done")
        c_ready = sem("c_ready")
        var_done = sem("var_done")
        up_done = sem("up_done")
        gate_ready = sem("gate_ready")
        gelu_done = sem("gelu_done")
        g_ready = sem("g_ready")
        g_turned = sem("g_turned")
        gT_ready = sem("gT_ready")
        y2_done = sem("y2_done")
        bb_ready = sem("bb_ready")
        ub_done = sem("ub_done")
        ub_ready = sem("ub_ready")
        in_r = sem("in_r")
        piece_full = sem("piece_full")
        piece_out = sem("piece_out")
        kn_ready = sem("kn_ready")
        kq_stored = sem("kq_stored")
        in_kq = sem("in_kq")
        k_spread = sem("k_spread")
        q_spread = sem("q_spread")
        keys_ready = sem("keys_ready")
        q_copied = sem("q_copied")
        qp_ready = sem("qp_ready")
        sq_ready = sem("sq_ready")
        state = sem("state")
        parts = [sem(f"parts{b}") for b in range(B)]
        arg_ready = sem("arg_ready")
        rdve = sem("rdve")
        gate_r = sem("gate_r")
        cell = sem("cell")
        cell_y = sem("cell_y")
        apart = {nc.tensor: sem("apart_pe"), nc.gpsimd: sem("apart_pool")}
        s_out = sem("s_out")
        fin = sem("fin")

        W_DMAS = 14
        C_DMAS = 5
        CONSTS = 8

        LINKS = {"sumsq": 4, "norm": 1 + 12, "cosine": 1, "mask": 1, "prob": 2, "var": 1 + 12}
        links_at, links_n = {}, 0
        for step in ORDER:
            links_at[step] = links_n
            links_n += LINKS.get(step[0], 0)
        links_at0, links_n0 = {}, 0
        for step in FIRST:
            links_at0[step] = links_n0
            links_n0 += LINKS.get(step[0], 0)
        LN_LINKS = 3 + 12
        D_N = LN_LINKS + links_n0 + links_n * ITERS
        D_BASE = [0, D_N + LN_LINKS]

        def nA(ph, i1, b):
            return i1 * 2 + (A_N * ph + b)

        def nB(ph, i, b):
            return i * 2 + (B_N * ph + b)

        def nC(ph, i, b):
            return i * 2 + (C_N * ph + b)

        def ring_base(ph, i):
            return i * RING_N + (R_N * ph + RING_N0)

        def earlier(name, step):
            return sum(s[0] == name for s in ORDER[:ORDER.index(step)])

        def loads_of(ph, l):
            return l * (16 * W_DMAS) + 16 * W_DMAS * (layers * ph + 1)

        def slot_of(i, b):
            return (i % POS) * B + b

        def par(i):
            return (i // POS) % 2

        kq_dram = nc.dram_tensor("kq_dram", [2, 4, T, GR, RN], F32, kind="Internal").ap()
        R_ITERS = T // UNROLL
        HALVES = UNROLL // BLOCK
        BCOLS = BLOCK * GR * RN
        QCOLS = GR * RN
        N_PIECES = [3, SLOTS // 4, SLOTS // 4, RG * SLOTS // 4, RG * SLOTS // 4, SLOTS]
        PIECE = [sum(N_PIECES[:n]) for n in range(len(N_PIECES) + 1)]
        R_DMAS = 8
        STORES = SLOTS // 2 * 2 * RG

        def wait_apart(eng, *waits):
            for sem_, v in waits:
                eng.wait_ge(sem_, v)
            eng.sem_inc(apart[eng], 1)

        def ffn_over(eng):
            eng.wait_ge(fin, 1)
            eng.wait_ge(rot_ready, C_N)
            eng.wait_ge(v_rest, 16 * A_N)
            eng.wait_ge(chunk_out, R_N)

        START = 1
        early = {nc.tensor: (y_done, y2_done, ub_done), nc.scalar: (oT_ready, fs_ready, keys_ready),
                 nc.vector: (s_read, p_ready, gate_ready, arg_ready),
                 nc.gpsimd: (qp_ready,)}

        block = ctx.enter_context(nc.Block())

        @block.sync
        def _(sp):
            def load_layer(l, half):
                def put(dst, src):
                    sp.dma_start(dst, src).then_inc(in_w, 16)
                at, ly = bass.ds(half, 1), bass.ds(l, 1)
                put(wqkv[:, at, :], Wqkv[ly].rearrange("l d n -> d l n"))
                put(wo[:, at, :, :].rearrange("p s k n -> p (s k) n"), Wo[ly].rearrange("l (k p) n -> p (l k) n", p=P))
                put(w1[:, at, :], W1[ly].rearrange("l d n -> d l n"))
                for j, (a, z) in enumerate(FF_CUTS):
                    put(w2[0:z - a, at, j, :], W2[ly, a:z, :].rearrange("l f n -> f l n"))
                put(b1r[:, at, :], b1[ly, :].unsqueeze(0))
                put(b2r[:, at, :], b2[ly, :].unsqueeze(0))
                h = DH // 2
                for j, vec in enumerate((q_scale, k_scale)):
                    put(scales[:, at, j, :], vec[ly, :].partition_broadcast(P))
                    put(scales[:, at, 2 + j, 0:h], vec[ly, h:DH].partition_broadcast(P))
                    put(scales[:, at, 2 + j, h:DH], vec[ly, 0:h].partition_broadcast(P))

            def v_shift(ph, i1, b, rb, first=False):
                n = nA(ph, i1, b)
                if first and ph == 0:
                    sp.wait_ge(consts, CONSTS)
                else:
                    sp.wait_ge(pv_done, nB(ph, i1 - 1, b) + 1)
                sp.dma_start(v_sh[0:WIN, b, :], v_al[P - WIN:P, b, :]).then_inc(v_edge, 16)
                sp.wait_ge(chunk_out, rb + 2)
                sp.dma_start(v_sh[WIN:P, b, :], v_al[0:P - WIN, b, :]).then_inc(v_rest, 16)

            for b in range(B):
                sp.dma_start(x_in[:, b::B, :], x[b].rearrange("(s t) d -> t s d", t=P)).then_inc(in_x, 16)
            sp.dma_start(ident[:, :], ident_in).then_inc(in_const, 16)
            sp.dma_start(rope_base[:, :, :, :], tables).then_inc(in_const, 16)
            sp.dma_start(masks[:, :, :], mask).then_inc(in_const, 16)
            with nc.allow_non_contiguous_dma("a few columns"):
                sp.dma_start(gcol[:, :], ln_g[0:layers].rearrange("l d -> d l")).then_inc(in_const, 16)
                sp.dma_start(bcol[:, :], ln_b[0:layers].rearrange("l d -> d l")).then_inc(in_const, 16)
            load_layer(0, 0)
            def recurrence():
                ffn_over(sp)
                sp.dma_start(w_raw[:, 0, :], W_in).then_inc(in_r, 16)
                for j, w in enumerate((W_k, W_q, W_v, W_beta)):
                    sp.dma_start(w_raw[:, 1 + 2 * j:3 + 2 * j, :], w.rearrange("(g m) d -> m g d", g=RG)).then_inc(in_r, 16)
                sp.dma_start(w_raw[:, 9:11, :], W_out.rearrange("d (g m) -> d g m", g=RG)).then_inc(in_r, 16)
                with nc.allow_non_contiguous_dma("two columns"):
                    sp.dma_start(beta_bias, b_beta.rearrange("(g h) n -> (h n) g", g=RG)).then_inc(in_r, 16)
                sp.dma_start(spread, spread_in).then_inc(in_r, 16)
                for hf in range(2):
                    sp.wait_ge(kn_ready, hf + 1)
                    for n in range(SLOTS // 2):
                        slot = hf * (SLOTS // 2) + n
                        ps, b = slot // B, slot % B
                        for a in range(2):
                            for g in range(RG):
                                sp.dma_start(kq_dram[a, :, ps * P:(ps + 1) * P, b * RG + g, :].rearrange("h t j -> t h j"),
                                             kq[:, n, a, g * P:(g + 1) * P].rearrange("t (h j) -> t h j", j=RN)
                                             ).then_inc(kq_stored, 16)
                kq_rows = kq_dram.rearrange("a h t g j -> h a (t g j)")

                def load(it):
                    sp.dma_start(kq_in[:, bass.ds(it % 2, 1), :, :].rearrange("h r a n -> h (r a) n"),
                                 kq_rows[:, :, bass.ds((it % R_ITERS) * (UNROLL * GR * RN), UNROLL * GR * RN)]).then_inc(in_kq, 16)
                sp.wait_ge(kq_stored, 16 * 2 * STORES)
                load(0)
                with sp.Fori(0, R_ITERS) as it:
                    sp.wait_ge(q_spread, it * HALVES + 1)
                    sp.wait_ge(in_kq, it * 16 + 16)
                    load(it + 1)

            for ph in range(phases):
                if ph:
                    recurrence()
                    sp.wait_ge(fin, 2)
                for step in FIRST:
                    if step[0] == "v":
                        v_shift(ph, 0, step[1], R_N * ph + RING_AT0[step], first=True)
                with sp.Fori(0, layers) as l:
                    sp.wait_ge(y2_done, l * (2 * POS) + B_N * ph + START)
                    load_layer((l + 1) % layers, (l + 1) % 2)
                    with sp.Fori(0, POS) as p:
                        i = l * POS + p
                        for step in ORDER:
                            if step[0] == "v":
                                v_shift(ph, i + 1, step[1], ring_base(ph, i) + RING_AT[step])
            sp.wait_ge(fin, 2 * phases - 1)
            for b in range(B):
                sp.dma_start(out[b].rearrange("(s t) d -> t s d", t=P), x_in[:, b::B, :]).then_inc(s_out, 16)
            sp.wait_ge(s_out, 16 * B)

        @block.gpsimd
        def _(pool):
            def rope(ph, i1, b, rb, first=False):
                n = nC(ph, i1, b)
                if b == 0:
                    pool.wait_ge(in_w, loads_of(ph, i1 // POS))
                    if not first:
                        pool.wait_ge(rot_ready, nC(ph, i1 - 1, 0) + 1)
                    elif ph:
                        pool.wait_ge(rot_ready, nC(ph, 0, 0))
                        pool.wait_ge(rs_ready, nC(ph, 0, 0) * 4)
                    pool.tensor_tensor(rope_tab[:, bass.ds(i1 % 2, 1)], rope_base[:, bass.ds(i1 % POS, 1)],
                                       scales[:, bass.ds(par(i1), 1)], ALU.mult).then_inc(rt_ready, 1)
                    pool.wait_ge(rt_ready, i1 + (ITERS + 1) * ph + 1)
                wait_apart(pool, (qn_ready, nA(ph, i1, b) + 1), *([] if first and ph == 0 and b == 0 else [(rot_ready, n)]))
                h = DH // 2
                src = qk[:, b, :].rearrange("p (t h d) -> p t h d", t=2, d=DH)
                dst = rot[:, :].rearrange("p (t h d) -> p t h d", t=2, d=DH)
                for a, z in ((0, h), (h, DH)):
                    for t in range(2):
                        tab = rope_tab[:, bass.ds(i1 % 2, 1), 2 + t, a:z].broadcast_to([P, HEADS, h])
                        pool.tensor_tensor(dst[:, t, :, a:z], src[:, t, :, h - a:DH - a], tab,
                                           ALU.mult).then_inc(rs_ready, 1)

            for signal in early[nc.gpsimd]:
                pool.sem_inc(signal, START)
            pool.memset(ones[:, :], 1.0).then_inc(consts, 1)
            pool.memset(kT[:, :, :, :], 0.0).then_inc(consts, 1)
            pool.memset(v_al[:, :, :], 0.0).then_inc(consts, 1)
            pool.memset(p_pad[:, :, :], 0.0).then_inc(consts, 1)
            pool.memset(xs[:, :, P:P + 2], 0.0).then_inc(consts, 1)
            pool.memset(fs[:, :, P:P + 2], 0.0).then_inc(consts, 1)
            pool.memset(mean_col[:, :], 1.0 / DIM).then_inc(consts, 1)
            pool.wait_ge(in_const, 16 * C_DMAS)
            pool.tensor_scalar(center[:, :], ident[:, :], 1.0 / DIM, None, ALU.subtract).then_inc(consts, 1)
            def recurrence():
                ffn_over(pool)
                pool.wait_ge(kq_stored, 16 * 2 * STORES)
                pool.memset(hist[:, :, :, 0:RN], 0.0).then_inc(state, 1)
                pool.memset(hist[:, :, :, RN:RN + 1], 1.0).then_inc(state, 1)
                pool.memset(qprod[:, 0, :, :], 0.0).then_inc(state, 1)
                pool.memset(queries[:, 1, :, :], 0.0).then_inc(q_copied, 1)

                def query(s):
                    pool.tensor_tensor(qprod[:, s % 2, :, :], hist[:, (s + BLOCK) % UNROLL, :, 0:RN], queries[:, s % 2, :, :],
                                       ALU.mult).then_inc(qp_ready, 1)

                with pool.Fori(0, R_ITERS) as it:
                    for s in range(UNROLL):
                        for b in range(B):
                            at = s * 2 + b
                            g = slice(b * RG, (b + 1) * RG)
                            wait_apart(pool, (state, it * (2 * UNROLL) + (at + 2)))
                            bt = beta[:, bass.ds(it * UNROLL + s, 1), g].rearrange("p t g -> p (t g)")
                            pool.tensor_tensor(decay[:, b, :, :], hist[:, (s - 1) % UNROLL, g, 0:RN],
                                               bt.unsqueeze(2).broadcast_to([P, RG, RN]), ALU.mult).then_inc(parts[b], 1)
                        wait_apart(pool, (q_copied, it * UNROLL + (s + 1)))
                        query((s - 1) % UNROLL)
                for s in range(-1, BLOCK):
                    pool.wait_ge(q_copied, T + s + 2)
                    pool.wait_ge(sq_ready, T + s + 1)
                    query(s % UNROLL)

            for ph in range(phases):
                if ph:
                    recurrence()
                for step in FIRST:
                    if step[0] == "cosine":
                        rope(ph, 0, step[1], 0, first=True)
                with pool.Fori(0, layers) as l:
                    with pool.Fori(0, POS) as p:
                        i = l * POS + p
                        for step in ORDER:
                            if step[0] == "cosine":
                                rope(ph, i + 1 if ahead(step) else i, step[1], 0)

        @block.tensor
        def _(pe):
            def ring_chunk(u, rb, c, emit):
                if not isinstance(rb, int) or rb + c >= 2:
                    pe.wait_ge(chunk_out, rb + (c - 1))
                emit(ring[(u + c) % 2]).then_inc(ring_full, 1)

            def turn(ph, i, b, rb, u, first=False, part=0):
                pe.wait_ge(rot_ready, nC(ph, i, b) + 1)
                for c in range(2):
                    def emit(bank):
                        for j in range(4):
                            at = (8 * part + 4 * c + j) * P
                            ins = pe.transpose(bank[:, j * P:(j + 1) * P], qk[:, b, at:at + P], ident[:, :])
                        return ins
                    ring_chunk(u, rb, c, emit)

            def score(ph, i, b, rb, u, first=False, part=0):
                if part == 0:
                    turned = max(RING_AT["turnq", b], RING_AT["turnk", b]) + 2
                    wait_apart(pe, (chunk_out, ring_base(ph, i) + turned),
                               (s_read, nB(ph, i, b) + START))
                for k in range(PAIRS // 2 * part, PAIRS // 2 * (part + 1)):
                    for w in range(P // WIN):
                        for e in range(2):
                            at = e * BANK + k * 2 * WIN
                            ins = pe.matmul(psS[w * WIN:(w + 1) * WIN, at:at + 2 * WIN],
                                            qT[e * DH:(e + 1) * DH, b, k, w * WIN:(w + 1) * WIN],
                                            kT[e * DH:(e + 1) * DH, b, k, w * WIN:(w + 2) * WIN],
                                            start=True, stop=True)
                if part == 1:
                    ins.then_inc(s_done, 1)

            def load(ph, i1, b, rb, u, first=False):
                n = nA(ph, i1, b)
                pe.wait_ge(x_copied, n + 1)
                if first:
                    pe.wait_ge(x_done, X_BASE[ph] + SLOTS)
                else:
                    pe.wait_ge(x_done, i1 * 2 + (X_BASE[ph] + SLOTS - 4 + b + 1))
                pe.transpose(psM[b][:, 0:P], xcur[:, b, :], ident[:, :]).then_inc(x_turned, 1)

            def project(ph, i1, b, rb, u, chunks, col):
                pe.wait_ge(xs_ready, nA(ph, i1, b) + 1)
                pe.wait_ge(in_w, loads_of(ph, i1 // POS))
                for c in range(chunks):
                    at = col + c * BANK
                    ring_chunk(u, rb, c, lambda bank: pe.matmul(
                        bank[:, :], xs[:, b, 0:P], wqkv[:, bass.ds(par(i1), 1), at:at + BANK], start=True, stop=True))

            def q_proj(ph, i1, b, rb, u, first=False):
                project(ph, i1, b, rb, u, 2, 0)

            def k_proj(ph, i1, b, rb, u, first=False):
                project(ph, i1, b, rb, u, 2, INNER)

            def v_proj(ph, i1, b, rb, u, first=False):
                project(ph, i1, b, rb, u, 2, 2 * INNER)

            def pturn(ph, i, b, rb, u, first=False, part=0):
                pe.wait_ge(p_ready, nB(ph, i, b) + 1 + START)
                for c in range(2):
                    def emit(bank):
                        for j in range(4):
                            ins = pe.transpose(bank[:, j * P:(j + 1) * P], p_pad[:, 8 * part + 4 * c + j, :], ident[:, :])
                        return ins
                    ring_chunk(u, rb, c, emit)

            def psO_free(ph, i, step):
                pe.wait_ge(oT_ready, nB(ph, i, 0) + earlier("pvb", step) + START)
                pe.wait_ge(gate_ready, nB(ph, i, 0) + earlier("up", step) + START)

            def pv(ph, i, b, rb, u, first=False, part=0):
                pe.wait_ge(chunk_out, rb_of(ph, i, ("pturnb" if part else "pturna", b)) + 2)
                pe.wait_ge(v_edge, (nA(ph, i, b) + 1) * 16)
                pe.wait_ge(v_rest, (nA(ph, i, b) + 1) * 16)
                pe.wait_ge(ub_ready, i // POS + (layers * ph + 1))
                if part == 0:
                    psO_free(ph, i, ("pva", b))
                o = psO[:, :].rearrange("p (k a w q) -> p k a w q", k=PAIRS, a=2, w=2)
                pr = pT[:, :, :].rearrange("p h (a w q) -> p h a w q", a=2, w=2)
                for k in range(PAIRS // 2 * part, PAIRS // 2 * (part + 1)):
                    for odd, v in ((1, v_al), (0, v_sh)):
                        for e in range(2):
                            at = (2 * k + e) * DH
                            ins = pe.matmul(o[e * DH:(e + 1) * DH, k, :, odd, :], v[:, b, at:at + DH],
                                            pr[:, 2 * k + e, :, odd, :], start=True, stop=True)
                if part == 1:
                    ins.then_inc(pv_done, 1)

            def out_proj(ph, i, b, rb, u, first=False):
                pe.wait_ge(oT_ready, nB(ph, i, b) + 1 + START)
                pe.wait_ge(xs_ready, nA(ph, i + 1, b) + 1)
                for k in range(PAIRS):
                    ins = pe.matmul(psM[b][:, 0:DIM], oT[:, k, :], wo[:, bass.ds(par(i), 1), k, :],
                                    start=(k == 0), stop=(k == PAIRS - 1))
                ins.then_inc(y_done, 1)

            def ln(ph, i, b, rb, u, first=False):
                pe.wait_ge(xmid_ready, nB(ph, i, b) + 1)
                pe.transpose(psM[b][:, 0:P], xmid[:, b, :], ident[:, :]).then_inc(m_turned, 1)

            def cent(ph, i, b, rb, u, first=False):
                pe.wait_ge(fs_ready, nB(ph, i, b) + 1 + START)
                pe.matmul(psM[b][:, 0:P], center[:, :], fs[:, b, 0:P], start=True, stop=True).then_inc(c_done, 1)

            def var(ph, i, b, rb, u, first=False):
                pe.wait_ge(c_ready, nB(ph, i, b) + 1)
                pe.matmul(psM[b][:, 0:1], csq[:, b, :], mean_col[:, :], start=True, stop=True).then_inc(var_done, 1)

            def up(ph, i, b, rb, u, first=False):
                psO_free(ph, i, ("up", b))
                for j in range(2):
                    ins = pe.matmul(psO[:, j * BANK:j * BANK + FF], cg[:, b, :],
                                    w1[:, bass.ds(par(i), 1), j * FF:(j + 1) * FF], start=True, stop=True)
                ins.then_inc(up_done, 1)

            def gturn(ph, i, b, rb, u, first=False):
                pe.wait_ge(g_ready, nB(ph, i, b) + 1)
                for j, (a, z) in enumerate(FF_CUTS):
                    ins = pe.transpose(psM[b][0:z - a, j * P:(j + 1) * P], ag[:, b, a:z], ident[:, :])
                ins.then_inc(g_turned, 1)

            def down(ph, i, b, rb, u, first=False):
                pe.wait_ge(gT_ready, nB(ph, i, b) + 1)
                for j, (a, z) in enumerate(FF_CUTS):
                    pe.matmul(psM[b][:, 0:DIM], gT[0:z - a, j, :], w2[0:z - a, bass.ds(par(i), 1), j, :],
                              start=(j == 0), stop=False)
                pe.matmul(psM[b][:, 0:DIM], ones[0:1, :], b2r[0:1, bass.ds(par(i), 1), :],
                          start=False, stop=True).then_inc(y2_done, 1)

            steps = {"turnq": turn, "turnk": partial(turn, part=1), "scorea": score, "scoreb": partial(score, part=1),
                     "load": load, "q": q_proj, "k": k_proj, "v": v_proj, "pturna": pturn,
                     "pturnb": partial(pturn, part=1), "pva": pv, "pvb": partial(pv, part=1), "wo": out_proj, "ln": ln, "cent": cent, "var": var, "up": up, "gturn": gturn,
                     "down": down}

            def rb_of(ph, i, step):
                return ring_base(ph, i) + RING_AT[step]

            def recurrence():
                ffn_over(pe)
                pe.wait_ge(in_r, 16 * R_DMAS)

                def piece(u, emit):
                    if u >= 2:
                        pe.wait_ge(piece_out, u - 1)
                    emit(ring[u % 2]).then_inc(piece_full, 1)

                def turned(srcs):
                    def emit(bank):
                        for j, src in enumerate(srcs):
                            ins = pe.transpose(bank[:, j * P:(j + 1) * P], src, ident[:, :])
                        return ins
                    return emit

                for n in range(N_PIECES[0]):
                    piece(n, turned([w_raw[:, j, :] for j in range(4 * n, min(4 * n + 4, 11))]))
                pe.wait_ge(x_done, X_N + SLOTS)
                for n in range(N_PIECES[1]):
                    piece(PIECE[1] + n, turned([x_tok[:, j, :] for j in range(4 * n, 4 * n + 4)]))
                pe.wait_ge(piece_out, PIECE[2])
                for n in range(N_PIECES[2]):
                    piece(PIECE[2] + n, lambda bank: pe.matmul(
                        bank[:, :], w_t[:, 0, :], xT[:, n * BANK:(n + 1) * BANK], start=True, stop=True))
                pe.wait_ge(piece_out, PIECE[3])
                for j, first in ((3, 5), (4, 7)):
                    for n in range(N_PIECES[j]):
                        g, c = n // (SLOTS // 4), n % (SLOTS // 4)
                        piece(PIECE[j] + n, lambda bank: pe.matmul(
                            bank[:, :], w_t[:, first + g, :], xpT[:, c * BANK:(c + 1) * BANK], start=True, stop=True))
                for n in range(N_PIECES[5]):
                    piece(PIECE[5] + n, lambda bank: pe.matmul(
                        bank[:, :], xpT[:, n * P:(n + 1) * P], w_t[:, 1:5, :].rearrange("p w m -> p (w m)"),
                        start=True, stop=True))

                def spread_block(a, it, hb, bank):
                    return pe.matmul(bank[:, :], spread[:, :],
                                     kq_in[:, bass.ds(it % 2, 1), a, hb * BCOLS:(hb + 1) * BCOLS],
                                     start=True, stop=True)

                pe.wait_ge(in_kq, 16)
                pe.wait_ge(piece_out, PIECE[6])
                for nb in range(HALVES):
                    spread_block(0, 0, nb, ring[nb]).then_inc(k_spread, 1)
                spread_block(1, 0, 0, psM[1]).then_inc(q_spread, 1)
                spread_block(1, 0, 0, psM[0]).then_inc(q_spread, 1)
                with pe.Fori(0, R_ITERS) as it:
                    for hb in range(HALVES):
                        if hb == 0:
                            pe.wait_ge(in_kq, it * 16 + 32)
                        pe.wait_ge(keys_ready, it * HALVES + (hb + 1) + START)
                        spread_block(0, it + 1, hb, ring[hb]).then_inc(k_spread, 1)
                        nxt, nb = (it, 1) if hb == 0 else (it + 1, 0)
                        pe.wait_ge(q_copied, (it * HALVES + (hb + 1)) * BLOCK + 1)
                        spread_block(1, nxt, nb, psM[nb]).then_inc(q_spread, 1)
                pe.wait_ge(cell, 1)
                for slot in range(SLOTS):
                    ps, b = slot // B, slot % B
                    bank = (psS, psO)[slot // (SLOTS // 2)]
                    at = slot % (SLOTS // 2) * DIM
                    for g in range(RG):
                        ins = pe.matmul(bank[:, at:at + DIM], sq[:, SQ_0 + ps * P:SQ_0 + (ps + 1) * P, b * RG + g],
                                        w_t[:, 9 + g, :], start=(g == 0), stop=(g == RG - 1))
                ins.then_inc(cell_y, 1)

            for signal in early[nc.tensor]:
                pe.sem_inc(signal, START)
            pe.wait_ge(consts, CONSTS)
            for ph in range(phases):
                if ph:
                    recurrence()
                for step in FIRST:
                    if step[0] in steps:
                        at = RING_AT0.get(step, 0)
                        steps[step[0]](ph, 0, step[1], R_N * ph + at, at, first=True)
                with pe.Fori(0, layers) as l:
                    pe.wait_ge(bb_ready, l + (layers * ph + 1))
                    pe.wait_ge(in_w, loads_of(ph, l))
                    pe.wait_ge(oT_ready, l * (2 * POS) + B_N * ph + START)
                    pe.wait_ge(gate_ready, l * (2 * POS) + B_N * ph + START)
                    for j in range(2):
                        half = bass.ds(l % 2, 1)
                        dst = psO[:, j * BANK:j * BANK + FF]
                        pe.matmul(dst, bbc[:, :], w1[:, half, j * FF:(j + 1) * FF], start=True, stop=False)
                        ins = pe.matmul(dst, ones[0:1, :], b1r[0:1, half, j * FF:(j + 1) * FF], start=False, stop=True)
                    ins.then_inc(ub_done, 1)
                    with pe.Fori(0, POS) as p:
                        i = l * POS + p
                        for step in ORDER:
                            if step[0] in steps:
                                at = RING_AT.get(step, 0)
                                i_of = i + 1 if ahead(step) else i
                                steps[step[0]](ph, i_of, step[1], ring_base(ph, i) + at, at)

        @block.scalar
        def _(act):
            def copy(dst, src, scale=1.0):
                return act.activation(dst, src, ACT.Copy, scale=scale)

            def carry_in(dst, b, p_at, sem_):
                copy(dst[DIM // 2:DIM, b, 0:1],
                     dst[DIM // 2:DIM, b, bass.ds((P + 1) - (p_at + POS - 1) // POS, 1)]).then_inc(sem_, 1)

            def shift_in(dst, b, bank, sem_):
                half = DIM // 2
                copy(dst[0:half, b, 0:P], bank[0:half, 0:P])
                copy(dst[half:DIM, b, 1:P + 1], bank[half:DIM, 0:P]).then_inc(sem_, 1)

            def load(ph, i1, b, rb, first=False):
                n = nA(ph, i1, b)
                act.wait_ge(x_done, i1 * 2 + (X_BASE[ph] + b + 1))
                if not (first and ph == 0):
                    act.wait_ge(x_turned, n - 1)
                copy(xcur[:, b, :], x_tok[:, bass.ds(slot_of(i1, b), 1), :]).then_inc(x_copied, 1)
                if not (first and ph == 0):
                    act.wait_ge(xs_ready, n - 1)
                carry_in(xs, b, i1 % POS, xs_carry)
                act.wait_ge(x_turned, n + 1)
                act.wait_ge(xs_carry, n + 1)
                shift_in(xs, b, psM[b], xs_ready)

            def qk_out(ph, i1, b, rb, first=False, part=0):
                n = nA(ph, i1, b)
                if not (first and ph == 0):
                    act.wait_ge(rot_ready, nC(ph, i1, b) - 1)
                for c in range(2):
                    at, bank = part * INNER + c * BANK, ring[(rb[1] + c) % 2]
                    act.wait_ge(ring_full, rb[0] + (c + 1))
                    copy(qk[:, b, at:at + BANK], bank[:, :])
                    act.activation(scr[:, b, at:at + BANK], bank[:, :], ACT.Square).then_inc(chunk_out, 1)

            def v_out(ph, i1, b, rb, first=False):
                act.wait_ge(v_edge, (nA(ph, i1, b) + 1) * 16)
                for c in range(2):
                    act.wait_ge(ring_full, rb[0] + (c + 1))
                    copy(v_al[:, b, c * BANK:(c + 1) * BANK], ring[(rb[1] + c) % 2][:, :]).then_inc(chunk_out, 1)

            def turn(ph, i, b, rb, first=False, part=0):
                if part == 1:
                    copy(kT[:, b, :, 0:WIN],
                         kT[:, b, :, bass.ds((P + WIN) - ((i % POS + POS - 1) // POS) * WIN, WIN)]).then_inc(tail_copied, 1)
                    act.wait_ge(tail_copied, nB(ph, i, b) + 1)
                for c in range(2):
                    act.wait_ge(ring_full, rb[0] + (c + 1))
                    src = ring[(rb[1] + c) % 2][:, :].rearrange("p (j t) -> p j t", t=P)
                    dst = (kT if part else qT)[:, b, 4 * c:4 * c + 4, part * WIN:part * WIN + P]
                    copy(dst, src).then_inc(chunk_out, 1)

            def soft(ph, i, b, rb, first=False):
                act.wait_ge(sub_done, nB(ph, i, b) + 1)
                act.activation(sm[:, :, :], sm[:, :, :], ACT.Exp).then_inc(exp_done, 1)

            def pturn(ph, i, b, rb, first=False, part=0):
                for c in range(2):
                    act.wait_ge(ring_full, rb[0] + (c + 1))
                    src = ring[(rb[1] + c) % 2][:, :].rearrange("p (j t) -> p j t", t=P)
                    copy(pT[:, 8 * part + 4 * c:8 * part + 4 * c + 4, :], src).then_inc(chunk_out, 1)

            def pv(ph, i, b, rb, first=False):
                act.wait_ge(pv_done, nB(ph, i, b) + 1)
                act.wait_ge(y_done, nB(ph, i, b) + START)
                copy(oT[:, :, :], psO[:, :].rearrange("p (k t) -> p k t", t=P)).then_inc(oT_ready, 1)

            def ln(ph, i, b, rb, first=False):
                n = nB(ph, i, b)
                act.wait_ge(fs_ready, n + START)
                carry_in(fs, b, i % POS, fs_carry)
                act.wait_ge(m_turned, n + 1)
                act.wait_ge(fs_carry, n + 1)
                shift_in(fs, b, psM[b], fs_ready)

            def cent(ph, i, b, rb, first=False):
                act.wait_ge(c_done, nB(ph, i, b) + 1)
                act.activation(csq[:, b, :], psM[b][:, 0:P], ACT.Square)
                copy(cg[:, b, :], psM[b][:, 0:P], gcol[:, bass.ds(i // POS, 1)]).then_inc(c_ready, 1)

            def up(ph, i, b, rb, first=False):
                act.wait_ge(gate_ready, nB(ph, i, b) + 1 + START)
                act.activation(ag[:, b, FF:2 * FF], ag[:, b, FF:2 * FF], ACT.Gelu).then_inc(gelu_done, 1)

            def gturn(ph, i, b, rb, first=False):
                act.wait_ge(g_turned, nB(ph, i, b) + 1)
                act.wait_ge(y2_done, nB(ph, i, 0) + earlier("down", ("gturn", b)) + START)
                last = FF_CUTS[-1][1] - FF_CUTS[-1][0]
                copy(gT[:, 0:2, :], psM[b][:, 0:2 * P].rearrange("p (j t) -> p j t", t=P))
                copy(gT[0:last, 2, :], psM[b][0:last, 2 * P:3 * P]).then_inc(gT_ready, 1)

            steps = {"load": load, "q": qk_out, "k": partial(qk_out, part=1), "v": v_out, "turnq": turn,
                     "turnk": partial(turn, part=1), "mask": soft, "pturna": pturn, "pturnb": partial(pturn, part=1),
                     "pvb": pv,
                     "ln": ln, "cent": cent, "up": up, "gturn": gturn}

            def recurrence():
                ffn_over(act)

                def piece(u):
                    act.wait_ge(piece_full, u + 1)
                    return ring[u % 2]

                for n in range(N_PIECES[0]):
                    k = min(4, 11 - 4 * n)
                    copy(w_t[:, 4 * n:4 * n + k, :], piece(n)[:, 0:k * P].rearrange("p (w m) -> p w m", m=P)
                         ).then_inc(piece_out, 1)
                for n in range(N_PIECES[1]):
                    copy(xT[:, n * BANK:(n + 1) * BANK], piece(PIECE[1] + n)[:, :]).then_inc(piece_out, 1)
                for n in range(N_PIECES[2]):
                    act.activation(xpT[:, n * BANK:(n + 1) * BANK], piece(PIECE[2] + n)[:, :], ACT.Silu
                                   ).then_inc(piece_out, 1)
                for j, dst in ((3, v_neg), (4, beta)):
                    for n in range(N_PIECES[j]):
                        g, c = n // (SLOTS // 4), n % (SLOTS // 4)
                        bank = piece(PIECE[j] + n)[:, :].rearrange("p (s b t) -> p s b t", b=B, t=P)
                        d = dst[:, c * (BANK // B):(c + 1) * (BANK // B), g::RG].rearrange("p (s t) b -> p s b t", t=P)
                        if j == 3:
                            ins = copy(d, bank, -1.0)
                        else:
                            ins = act.activation(d, bank, ACT.Sigmoid, bias=beta_bias[:, g:g + 1])
                        ins.then_inc(piece_out, 1)
                for n in range(N_PIECES[5]):
                    if n == SLOTS // 2:
                        act.wait_ge(kq_stored, 16 * STORES)
                    copy(kq[:, n % (SLOTS // 2), :, :], piece(PIECE[5] + n)[:, :].rearrange("p (a m) -> p a m", a=2)
                         ).then_inc(piece_out, 1)

                def keys_out(n_of, it, hb, first=False):
                    act.wait_ge(k_spread, n_of + 1)
                    if not first:
                        act.wait_ge(arg_ready, (n_of - 1) * (2 * BLOCK) + START)
                    ks = slice(hb * BLOCK, (hb + 1) * BLOCK)
                    copy(keys[:, ks, :, 0:RN].rearrange("p t g j -> p (t g) j"), ring[hb][:, :].rearrange("p (n j) -> p n j", j=RN))
                    copy(keys[:, ks, :, RN],
                         v_neg[:, bass.ds(it * UNROLL + hb * BLOCK, BLOCK), :]).then_inc(keys_ready, 1)

                def queries_out(n_of, hb, k):
                    if k == 0:
                        act.wait_ge(q_spread, n_of + 1)
                    copy(queries[:, k % 2, :, :].rearrange("p g j -> p (g j)"),
                         psM[1 - hb][:, k * QCOLS:(k + 1) * QCOLS]).then_inc(q_copied, 1)

                act.wait_ge(state, 3)
                keys_out(0, 0, 0, first=True)
                with act.Fori(0, R_ITERS) as it:
                    for hb in range(HALVES):
                        for s in range(hb * BLOCK, (hb + 1) * BLOCK):
                            for b in range(B):
                                act.wait_ge(arg_ready, it * (2 * UNROLL) + (2 * s + b + 1) + START)
                                act.activation(hist[:, s, b * RG:(b + 1) * RG, 0:RN], arg[:, b, :, :], ACT.Tanh
                                               ).then_inc(state, 1)
                                if b == 0:
                                    queries_out(it * HALVES + hb, hb, s - hb * BLOCK)
                                    if s == 0:
                                        keys_out(it * HALVES + 1, it, 1)
                                    elif s == BLOCK:
                                        keys_out(it * HALVES + 2, (it + 1) % R_ITERS, 0)
                for k in range(BLOCK):
                    act.wait_ge(qp_ready, T + k + START)
                    queries_out(R_ITERS * HALVES, 0, k)
                act.wait_ge(sq_ready, T + SQ_0)
                act.wait_ge(q_spread, R_ITERS * HALVES + 2)
                act.wait_ge(in_kq, 16 * (R_ITERS + 1))
                act.activation(gate, sq[:, SQ_0:, :], ACT.Sigmoid).then_inc(gate_r, 1)

            for signal in early[nc.scalar]:
                act.sem_inc(signal, START)
            act.wait_ge(consts, CONSTS)
            for ph in range(phases):
                if ph:
                    recurrence()
                for step in FIRST:
                    if step[0] in steps:
                        at = RING_AT0.get(step, 0)
                        steps[step[0]](ph, 0, step[1], (R_N * ph + at, at), first=True)
                with act.Fori(0, layers) as l:
                    act.wait_ge(ub_done, l + layers * ph + START)
                    act.activation(bbc[:, :], ones[:, :], ACT.Copy, scale=bcol[:, bass.ds(l, 1)]).then_inc(bb_ready, 1)
                    act.wait_ge(ub_done, l + (layers * ph + 1) + START)
                    act.wait_ge(gate_ready, l * (2 * POS) + B_N * ph + START)
                    copy(up_bias[:, :].rearrange("p (j f) -> p j f", j=2),
                         psO[:, :].rearrange("p (j f) -> p j f", j=2)[:, :, 0:FF]).then_inc(ub_ready, 1)
                    with act.Fori(0, POS) as p:
                        i = l * POS + p
                        for step in ORDER:
                            if step[0] in steps:
                                at = RING_AT.get(step, 0)
                                i_of = i + 1 if ahead(step) else i
                                steps[step[0]](ph, i_of, step[1], (ring_base(ph, i) + at, at))

        @block.vector
        def _(dv):
            chain = [0, 0]
            chain_sem = [dve]

            def link(ins):
                chain[1] += 1
                ins.then_inc(chain_sem[0], 1)
                dv.wait_ge(chain_sem[0], chain[0] + chain[1])

            def rsqrt(dst, src, n, nt=nt):
                y, t, h = nt[:, 0, 0:n], nt[:, 1, 0:n], nt[:, 2, 0:n]
                link(dv.tensor_scalar(t.bitcast(U32), src.bitcast(U32), 1, None, ALU.logical_shift_right))
                link(dv.tensor_scalar(y.bitcast(I32), t.bitcast(I32), -1.0, RSQRT_MAGIC, ALU.mult, ALU.add))
                link(dv.tensor_scalar(h, src, -0.5, None, ALU.mult))
                for r in range(3):
                    link(dv.tensor_tensor(t, y, y, ALU.mult))
                    link(dv.tensor_tensor(t, t, h, ALU.mult))
                    link(dv.scalar_tensor_tensor(out=dst if r == 2 else y, in0=t, scalar=1.5, in1=y,
                                                 op0=ALU.add, op1=ALU.mult))

            def sumsq(ph, i1, b, rb, first=False):
                for c in range(4):
                    dv.wait_ge(chunk_out, rb[c // 2] + (c % 2 + 1))
                    ins = dv.tensor_reduce(ss[:, b, 8 * c:8 * c + 8],
                                           scr[:, b, c * BANK:(c + 1) * BANK].rearrange("p (h d) -> p h d", d=DH),
                                           AX_X, ALU.add)
                    link(ins)

            def norm(ph, i1, b, rb, first=False):
                link(dv.tensor_scalar(ss[:, b, :], ss[:, b, :], 1e-24, None, ALU.max))
                rsqrt(ss[:, b, :], ss[:, b, :], 2 * HEADS)
                q = qk[:, b, :].rearrange("p (h d) -> p h d", d=DH)
                dv.tensor_tensor(q, q, ss[:, b, :].unsqueeze(2).broadcast_to([P, 2 * HEADS, DH]),
                                 ALU.mult).then_inc(qn_ready, 1)

            def cosine(ph, i1, b, rb, first=False):
                n = nC(ph, i1, b)
                dv.wait_ge(rt_ready, i1 + ((ITERS + 1) * ph + 1))
                dv.wait_ge(qn_ready, nA(ph, i1, b) + 1)
                for t in range(2):
                    tab = rope_tab[:, bass.ds(i1 % 2, 1), t, :].broadcast_to([P, HEADS, DH])
                    cols = slice(t * INNER, (t + 1) * INNER)
                    ins = dv.tensor_tensor(scr[:, b, cols].rearrange("p (h d) -> p h d", d=DH),
                                           qk[:, b, cols].rearrange("p (h d) -> p h d", d=DH), tab, ALU.mult)
                link(ins)

            def rope(ph, i1, b, rb, first=False):
                n = nC(ph, i1, b)
                dv.wait_ge(rs_ready, (n + 1) * 4)
                dv.tensor_tensor(qk[:, b, :], scr[:, b, :], rot[:, :], ALU.add).then_inc(rot_ready, 1)

            def mask_(ph, i, b, rb, first=False):
                n = nB(ph, i, b)
                dv.wait_ge(s_done, n + 1)
                dv.wait_ge(p_ready, n + START)
                hd = sm[:, :, :]
                dv.tensor_tensor(hd, psS[:, :].rearrange("p (h j) -> p h j", j=2 * WIN),
                                 masks[:, bass.ds((i % POS + POS - 1) // POS, 1), :].broadcast_to([P, HEADS, 2 * WIN]),
                                 ALU.add).then_inc(s_read, 1)
                dv.wait_ge(s_read, n + 1 + START)
                link(dv.tensor_reduce(mx[:, :], hd, AX_X, ALU.max))
                dv.tensor_tensor(hd, hd, mx[:, :].unsqueeze(2).broadcast_to([P, HEADS, 2 * WIN]),
                                 ALU.subtract).then_inc(sub_done, 1)

            def prob(ph, i, b, rb, first=False):
                hd = sm[:, :, :]
                dv.wait_ge(exp_done, nB(ph, i, b) + 1)
                link(dv.tensor_reduce(rl[:, :], hd, AX_X, ALU.add))
                link(dv.reciprocal(rl[:, :], rl[:, :]))
                if b == 0:
                    dv.wait_ge(ring_full, ring_base(ph, i) + (RING_AT["pturnb", 1] + 2 - RING_N))
                else:
                    dv.wait_ge(ring_full, ring_base(ph, i) + (RING_AT["pturnb", 0] + 2))
                half = P // 2
                for a, z in ((0, half), (half, P)):
                    ins = dv.tensor_tensor(p_pad[a:z, :, a:z].rearrange("p (k e) j -> p e k j", e=2),
                                           sm[a:z, :, :].rearrange("p (e k) j -> p e k j", e=2),
                                           rl[a:z, :].rearrange("p (e k) -> p e k", e=2).unsqueeze(3).broadcast_to(
                                               [half, 2, PAIRS, half]), ALU.mult)
                ins.then_inc(p_ready, 1)

            def out_proj(ph, i, b, rb, first=False):
                dv.wait_ge(y_done, nB(ph, i, b) + 1 + START)
                dv.tensor_tensor(xmid[:, b, :], psM[b][:, 0:DIM], x_tok[:, bass.ds(slot_of(i, b), 1), :].squeeze(1),
                                 ALU.add).then_inc(xmid_ready, 1)

            def var(ph, i, b, rb, first=False):
                dv.wait_ge(var_done, nB(ph, i, b) + 1)
                link(dv.tensor_scalar(rstd[:, b:b + 1], psM[b][:, 0:1], LN_EPS, None, ALU.add))
                rsqrt(rstd[:, b:b + 1], rstd[:, b:b + 1], 1)

            def up(ph, i, b, rb, first=False):
                n = nB(ph, i, b)
                dv.wait_ge(up_done, n + 1)
                for j in range(2):
                    ins = dv.scalar_tensor_tensor(out=ag[:, b, j * FF:(j + 1) * FF], in0=psO[:, j * BANK:j * BANK + FF],
                                                  scalar=rstd[:, b:b + 1], in1=up_bias[:, j * FF:(j + 1) * FF],
                                                  op0=ALU.mult, op1=ALU.add)
                ins.then_inc(gate_ready, 1)

            def gate_mul(ph, i, b, rb, first=False):
                dv.wait_ge(gelu_done, nB(ph, i, b) + 1)
                dv.tensor_tensor(ag[:, b, 0:FF], ag[:, b, 0:FF], ag[:, b, FF:2 * FF], ALU.mult).then_inc(g_ready, 1)

            def down(ph, i, b, rb, first=False):
                dv.wait_ge(y2_done, nB(ph, i, b) + 1 + START)
                dv.tensor_tensor(x_tok[:, bass.ds(slot_of(i, b), 1), :].squeeze(1), psM[b][:, 0:DIM], xmid[:, b, :],
                                 ALU.add).then_inc(x_done, 1)

            steps = {"sumsq": sumsq, "norm": norm, "cosine": cosine, "rope": rope, "mask": mask_, "prob": prob,
                     "wo": out_proj, "var": var, "up": up, "gate": gate_mul, "down": down}

            def run(step, ph, i, rb, base, first=False):
                chain[0], chain[1] = base, 0
                steps[step[0]](ph, i, step[1], rb, first)
                assert chain[1] == LINKS.get(step[0], 0), (step, chain[1])

            def layernorm(ph, base):
                chain[0], chain[1] = base, 0
                for s in range(SLOTS):
                    ins = dv.bn_stats(stats[:, s, :], x_in[:, s, :])
                link(ins)
                for s in range(SLOTS):
                    ins = dv.bn_aggr(mv[:, s, :], stats[:, s, :])
                link(ins)
                link(dv.tensor_scalar(rs16[:, :], mv[:, :, 1], LN_EPS, None, ALU.add))
                rsqrt(rs16[:, :], rs16[:, :], SLOTS)
                for s in range(SLOTS):
                    dv.tensor_scalar(x_tok[:, s, :], x_in[:, s, :], mv[:, s, 0:1], rs16[:, s:s + 1],
                                     ALU.subtract, ALU.mult).then_inc(x_done, 1)

            def recurrence():
                ffn_over(dv)
                layernorm(0, D_N)
                chain[0], chain[1], chain_sem[0] = 0, 0, rdve
                rows = SLOTS // 2 * RH
                for hf in range(2):
                    dv.wait_ge(piece_out, PIECE[5] + (hf + 1) * (SLOTS // 2))
                    k = kq[:, :, 0, :]
                    link(dv.tensor_tensor(ksq, k, k, ALU.mult))
                    link(dv.tensor_reduce(knorm, ksq.rearrange("p s (h j) -> p (s h) j", j=RN), AX_X, ALU.add))
                    rsqrt(ksq[:, 0, 0:rows], knorm, rows, nt_r)
                    link(dv.tensor_tensor(knorm, knorm, ksq[:, 0, 0:rows], ALU.mult))
                    link(dv.tensor_scalar(knorm, knorm, 1e-6, None, ALU.add))
                    link(dv.reciprocal(knorm, knorm))
                    for n in range(SLOTS // 2):
                        kn = k[:, n, :].rearrange("p (h j) -> p h j", j=RN)
                        ins = dv.tensor_tensor(kn, kn, knorm[:, n * RH:(n + 1) * RH].unsqueeze(2).broadcast_to([P, RH, RN]),
                                               ALU.mult)
                    ins.then_inc(kn_ready, 1)
                base = chain[1]
                dv.wait_ge(kq_stored, 16 * 2 * STORES)

                def query_sum(t, s):
                    dv.wait_ge(qp_ready, t + START)
                    dv.tensor_reduce(sq[:, bass.ds(t, 1), :].rearrange("p t g -> p (t g)"), qprod[:, s % 2, :, :],
                                     AX_X, ALU.add).then_inc(sq_ready, 1)

                of_seq = [slice(b * RG, (b + 1) * RG) for b in range(B)]

                def product(b, s, state_at):
                    dv.wait_ge(state, state_at)
                    dv.tensor_tensor(prod[:, b, :, :], hist[:, (s - 1) % UNROLL, of_seq[b], :],
                                     keys[:, s % UNROLL, of_seq[b], :], ALU.mult).then_inc(rdve, 1)

                def product_sum(b, at):
                    dv.wait_ge(rdve, at)
                    dv.tensor_reduce(nd[:, b, :], prod[:, b, :, :], AX_X, ALU.add).then_inc(rdve, 1)

                def update(b, s, at):
                    dv.wait_ge(rdve, at)
                    dv.tensor_tensor(upd[:, b, :, :], keys[:, s, of_seq[b], 0:RN],
                                     nd[:, b, :].unsqueeze(2).broadcast_to([P, RG, RN]), ALU.mult).then_inc(parts[b], 1)

                def argument(b, at):
                    dv.wait_ge(parts[b], at)
                    dv.tensor_tensor(arg[:, b, :, :], decay[:, b, :, :], upd[:, b, :, :],
                                     ALU.subtract).then_inc(arg_ready, 1)

                dv.wait_ge(keys_ready, 1 + START)
                product(0, 0, 2)
                product_sum(0, base + 1)
                base += 2
                per = 4
                with dv.Fori(0, R_ITERS) as it:
                    for s in range(UNROLL):
                        hb, k, at = s // BLOCK, s % BLOCK, it * (per * UNROLL) + (base + per * s)
                        t = it * UNROLL + s
                        update(0, s, at)
                        argument(0, (t + 1) * 2)
                        product(1, s, it * (2 * UNROLL) + (2 * s + 3))
                        query_sum(t, s)
                        product_sum(1, at + 1)
                        if k == BLOCK - 1:
                            dv.wait_ge(keys_ready, it * HALVES + (hb + 2) + START)
                        product(0, s + 1, it * (2 * UNROLL) + (2 * s + 4))
                        update(1, s, at + 2)
                        product_sum(0, at + 3)
                        argument(1, (t + 1) * 2)
                dv.wait_ge(state, 2 * T + 3)
                for s in range(SQ_0):
                    query_sum(T + s, s)
                dv.wait_ge(sq_ready, T + SQ_0)
                chain[0], chain[1] = base + per * T, 0
                g1, s1 = gate.rearrange("p t g -> p (t g)"), sq[:, SQ_0:, :].rearrange("p t g -> p (t g)")
                dv.wait_ge(gate_r, 1)
                link(dv.tensor_tensor(g1, g1, s1, ALU.mult))
                dv.tensor_tensor(s1, g1, s1, ALU.mult).then_inc(cell, 1)
                dv.wait_ge(cell_y, 1)
                for n, bank in enumerate((psS, psO)):
                    xi = x_in[:, n * (SLOTS // 2):(n + 1) * (SLOTS // 2), :].rearrange("p s d -> p (s d)")
                    ins = dv.tensor_tensor(xi, xi, bank[:, :], ALU.add)
                chain_sem[0], chain[0], chain[1] = fin, 1, 0
                link(ins)
                chain_sem[0] = dve

            for signal in early[nc.vector]:
                dv.sem_inc(signal, START)
            dv.wait_ge(in_x, 16 * B)
            for ph in range(phases):
                if ph:
                    recurrence()
                layernorm(ph, D_BASE[ph])
                base0 = D_BASE[ph] + LN_LINKS
                for step in FIRST:
                    if step[0] in steps:
                        rb = [R_N * ph + RING_AT0[n, step[1]] for n in "qk"]
                        run(step, ph, 0, rb, base0 + links_at0[step], first=True)
                with dv.Fori(0, layers) as l:
                    with dv.Fori(0, POS) as p:
                        i = l * POS + p
                        for step in ORDER:
                            if step[0] in steps:
                                i_of = i + 1 if ahead(step) else i
                                rb = [ring_base(ph, i) + RING_AT[n, step[1]] for n in "qk"]
                                run(step, ph, i_of, rb, i * links_n + (base0 + links_n0 + links_at[step]))
                dv.wait_ge(x_done, X_BASE[ph] + X_N)
                dv.scalar_tensor_tensor(out=x_in[:, :, :].rearrange("p s d -> p (s d)"),
                                        in0=x_tok[:, :, :].rearrange("p s d -> p (s d)"), scalar=0.5,
                                        in1=x_in[:, :, :].rearrange("p s d -> p (s d)"),
                                        op0=ALU.mult, op1=ALU.add).then_inc(fin, 1)
                dv.wait_ge(fin, 2 * ph + 1)


def rope_tables(n):
    half = np.arange(0, DH, 2, dtype=np.float32)
    inv_freq = (np.float32(1.0) / np.power(np.float32(10000.0), half / np.float32(DH))).astype(np.float32)
    t = np.arange(n, dtype=np.float32)
    freqs = t[:, None] * inv_freq[None, :]
    freqs = np.concatenate([freqs, freqs], -1)
    base = (half + np.float32(0.4 * DH)) / np.float32(1.4 * DH)
    power = (t - np.float32(n // 2)) / np.float32(WIN // 2)
    scale = np.power(base[None, :], power[:, None])
    scale = np.concatenate([scale, scale], -1)
    cos, sin = np.cos(freqs), np.sin(freqs)
    sin = sin * np.where(np.arange(DH) < DH // 2, np.float32(-1), np.float32(1))[None, :]
    qk_scale = np.float32(8.0)
    tabs = np.stack([qk_scale * cos * scale, cos / scale, qk_scale * sin * scale, sin / scale], 1)
    return np.ascontiguousarray(tabs.reshape(n // P, P, 4, DH).transpose(1, 0, 2, 3)).astype(np.float32)


def window_masks():
    q = np.arange(P)
    c = np.arange(2 * WIN)[None, :]
    far = (c > (q % WIN)[:, None] + WIN) | (c < (q % WIN)[:, None])
    edge = far | ((q < WIN)[:, None] & (c < WIN))
    return (np.stack([edge, far], 1) * -np.finfo(np.float32).max).astype(np.float32)


def spread_matrix():
    return np.repeat(np.eye(P // RN, dtype=np.float32), RN, axis=1)


def kernel(**inputs):
    import concourse.bacc as bacc
    from concourse.bass_utils import run_bass_kernel_spmd

    arrays = {n: np.ascontiguousarray(inputs["L0_" + n]) for n in (
        "attn_x", "attn_W_in", "attn_W_k", "attn_W_v", "attn_W_q", "attn_W_beta", "attn_b_beta", "attn_W_out",
        "ffn_Wqkv", "ffn_q_scale", "ffn_k_scale", "ffn_Wo", "ffn_ln_g", "ffn_ln_b", "ffn_W1", "ffn_b1", "ffn_W2",
        "ffn_b2")}
    shape = arrays["attn_x"].shape
    arrays["tables"] = rope_tables(shape[1])
    arrays["mask"] = window_masks()
    arrays["ident_in"] = np.eye(P, dtype=np.float32)
    arrays["spread_in"] = spread_matrix()
    nc = bacc.Bacc("TRN2", target_bir_lowering=False, num_devices=1)
    aps = {n.removeprefix("attn_").removeprefix("ffn_"):
           nc.dram_tensor(f"in_{n}", a.shape, mybir.dt.from_np(a.dtype), kind="ExternalInput").ap()
           for n, a in arrays.items()}
    out = nc.dram_tensor("out_x", shape, F32, kind="ExternalOutput").ap()
    build(nc, out=out, **aps)
    r = run_bass_kernel_spmd(nc, [{f"in_{n}": a for n, a in arrays.items()}], core_ids=[0])
    return r.results[0]["out_x"]
```
